# Optimizing a Trainium2 kernel written in Bass

```python
import numpy as np
import jax
import jax.numpy as jnp

def _softmax(x, axis=-1):
    return jax.nn.softmax(x, axis=axis)

def _gelu(x):
    return jax.nn.gelu(x, approximate=True)

def _silu(x):
    return jax.nn.silu(x)

def _sigmoid(x):
    return jax.nn.sigmoid(x)

def _layernorm(x, axis=-1, eps=1e-05):
    m = jnp.mean(x, axis=axis, keepdims=True)
    v = jnp.var(x, axis=axis, keepdims=True)
    return (x - m) / jnp.sqrt(v + eps)

def _scatter_add(tgt, idx, src, axis=0):
    return tgt.at[idx].add(src)

def _segment_sum(src, seg, n):
    return jax.ops.segment_sum(src, seg, n)
kernel_name = 'mk_gnn_resnorm_d2_gnn_r16_2d2423'

def setup_inputs(seed: int=0):
    np.random.seed(seed)
    _w = jnp.asarray

    def _rec_inputs():
        import jax
        import jax.numpy as jnp
        _gk = jax.random.key(seed)
        x = -0.000202 + 1 * jax.random.normal(jax.random.fold_in(_gk, 1), (6250, 128), jnp.float32)
        _s = jax.random.randint(jax.random.fold_in(_gk, 2), (100000,), 0, 6250, jnp.int32)
        _d = jax.random.randint(jax.random.fold_in(_gk, 3), (100000,), 0, 6250, jnp.int32)
        _loop = jnp.arange(6250, dtype=jnp.int32)
        src = jnp.concatenate([_s, _d, _loop])
        dst = jnp.concatenate([_d, _s, _loop])
        _o = jnp.argsort(dst, stable=True)
        src = src[_o]
        dst = dst[_o]
        edge_weight = jax.random.uniform(jax.random.fold_in(_gk, 13), (206250,), jnp.float32, 0.0, 0.999998)
        return (x, src, dst, edge_weight)
    x, src, dst, edge_weight = _rec_inputs()

    def _L0_gnn_setup():
        import jax, jax.numpy as jnp
        import numpy as np
        N_NODES = 3125
        N_EDGES = 50000
        C_IN = 128
        HID = 128
        C_OUT = 128

        def _glorot(key, shape):
            fan_in, fan_out = shape
            lim = (6.0 / (fan_in + fan_out)) ** 0.5
            return jax.random.uniform(key, shape, jnp.float32, -lim, lim)

        def _edge_conv(x, src, dst, W1, b1, W2, b2, n_nodes):
            xi = x[dst]
            xj = x[src]
            m = jnp.concatenate([xi, xj - xi], axis=-1)
            h = jax.nn.relu(m @ W1 + b1) @ W2 + b2
            agg = jax.ops.segment_max(h, dst, num_segments=n_nodes)
            return jnp.where(jnp.isfinite(agg), agg, 0.0)
        key = jax.random.key(seed)
        ks = jax.random.split(key, 8)
        x = jax.random.normal(ks[0], (N_NODES, C_IN), jnp.float32)
        edge_index = jax.random.randint(ks[1], (2, N_EDGES), 0, N_NODES, jnp.int32)
        return {'x': x, 'edge_index': edge_index, 'W1_in': _glorot(ks[2], (2 * C_IN, HID)), 'b1_in': jnp.zeros((HID,), jnp.float32), 'W2_in': _glorot(ks[3], (HID, HID)), 'b2_in': jnp.zeros((HID,), jnp.float32), 'W1_hid': _glorot(ks[4], (2 * HID, HID)), 'b1_hid': jnp.zeros((HID,), jnp.float32), 'W2_hid': _glorot(ks[5], (HID, HID)), 'b2_hid': jnp.zeros((HID,), jnp.float32), 'W1_out': _glorot(ks[6], (2 * HID, HID)), 'b1_out': jnp.zeros((HID,), jnp.float32), 'W2_out': _glorot(ks[7], (HID, C_OUT)), 'b2_out': jnp.zeros((C_OUT,), jnp.float32)}
    _L0_gnn_all = _L0_gnn_setup()
    _L0_gnn_in = {k: v for k, v in _L0_gnn_all.items() if k in ('W1_in', 'b1_in', 'W2_in', 'b2_in', 'W1_hid', 'b1_hid', 'W2_hid', 'b2_hid', 'W1_out', 'b1_out', 'W2_out', 'b2_out')}
    del _L0_gnn_all

    def _L1_gnn_setup():
        import jax, jax.numpy as jnp
        import numpy as np
        N_NODES = 3125
        N_EDGES = 50000
        D = 128
        key = jax.random.key(seed)
        k1, k2, k3, k4, k5 = jax.random.split(key, 5)
        h = jax.random.normal(k1, (N_NODES, D), dtype=jnp.float32)
        gain = 1.414
        bound = gain * float(np.sqrt(6.0 / (2 * D + 1)))
        att = jax.random.uniform(k2, (2 * D, 1), dtype=jnp.float32, minval=-bound, maxval=bound)
        adj_values = jax.random.uniform(k3, (N_EDGES,), dtype=jnp.float32)
        row = jax.random.randint(k4, (N_EDGES,), 0, N_NODES, dtype=jnp.int64)
        col = jax.random.randint(k5, (N_EDGES,), 0, N_NODES, dtype=jnp.int64)
        return {'h': h, 'att': att, 'adj_values': adj_values, 'row': row, 'col': col}
    _L1_gnn_all = _L1_gnn_setup()
    _L1_gnn_in = {k: v for k, v in _L1_gnn_all.items() if k in ('att',)}
    del _L1_gnn_all
    return {'x': x, 'src': src, 'dst': dst, 'edge_weight': edge_weight, 'L0_gnn_W1_in': _L0_gnn_in['W1_in'], 'L0_gnn_b1_in': _L0_gnn_in['b1_in'], 'L0_gnn_W2_in': _L0_gnn_in['W2_in'], 'L0_gnn_b2_in': _L0_gnn_in['b2_in'], 'L0_gnn_W1_hid': _L0_gnn_in['W1_hid'], 'L0_gnn_b1_hid': _L0_gnn_in['b1_hid'], 'L0_gnn_W2_hid': _L0_gnn_in['W2_hid'], 'L0_gnn_b2_hid': _L0_gnn_in['b2_hid'], 'L0_gnn_W1_out': _L0_gnn_in['W1_out'], 'L0_gnn_b1_out': _L0_gnn_in['b1_out'], 'L0_gnn_W2_out': _L0_gnn_in['W2_out'], 'L0_gnn_b2_out': _L0_gnn_in['b2_out'], 'L1_gnn_att': _L1_gnn_in['att']}

def reference(x, src, dst, edge_weight, L0_gnn_W1_in, L0_gnn_b1_in, L0_gnn_W2_in, L0_gnn_b2_in, L0_gnn_W1_hid, L0_gnn_b1_hid, L0_gnn_W2_hid, L0_gnn_b2_hid, L0_gnn_W1_out, L0_gnn_b1_out, L0_gnn_W2_out, L0_gnn_b2_out, L1_gnn_att):
    import jax
    import jax.numpy as jnp

    def _L0_gnn_ref(x, edge_index, W1_in, b1_in, W2_in, b2_in, W1_hid, b1_hid, W2_hid, b2_hid, W1_out, b1_out, W2_out, b2_out):
        import jax, jax.numpy as jnp
        import numpy as np
        N_NODES = 3125
        N_EDGES = 50000
        C_IN = 128
        HID = 128
        C_OUT = 128

        def _glorot(key, shape):
            fan_in, fan_out = shape
            lim = (6.0 / (fan_in + fan_out)) ** 0.5
            return jax.random.uniform(key, shape, jnp.float32, -lim, lim)

        def _edge_conv(x, src, dst, W1, b1, W2, b2, n_nodes):
            xi = x[dst]
            xj = x[src]
            m = jnp.concatenate([xi, xj - xi], axis=-1)
            h = jax.nn.relu(m @ W1 + b1) @ W2 + b2
            agg = jax.ops.segment_max(h, dst, num_segments=n_nodes)
            return jnp.where(jnp.isfinite(agg), agg, 0.0)
        src, dst = (edge_index[0], edge_index[1])
        n = x.shape[0]
        x = _edge_conv(x, src, dst, W1_in, b1_in, W2_in, b2_in, n)
        x = jax.nn.relu(x)
        x = _edge_conv(x, src, dst, W1_hid, b1_hid, W2_hid, b2_hid, n)
        x = jax.nn.relu(x)
        x = _edge_conv(x, src, dst, W1_out, b1_out, W2_out, b2_out, n)
        return x

    def _L1_gnn_ref(h, att, adj_values, row, col):
        import jax, jax.numpy as jnp
        import numpy as np
        N_NODES = 3125
        N_EDGES = 50000
        D = 128
        d = h.shape[1]
        s = (h @ att[:d]).squeeze(1)
        t = (h @ att[d:]).squeeze(1)
        e = s[row] + t[col]
        e = jax.nn.leaky_relu(e, negative_slope=0.2)
        a = jax.nn.softmax(e, axis=0)
        w = adj_values * a
        msgs = w[:, None] * h[col]
        h_prime = jax.ops.segment_sum(msgs, row, num_segments=h.shape[0])
        return h_prime
    edge_index = jnp.stack([src, dst])
    x = _layernorm(x + _L0_gnn_ref(x, edge_index, L0_gnn_W1_in, L0_gnn_b1_in, L0_gnn_W2_in, L0_gnn_b2_in, L0_gnn_W1_hid, L0_gnn_b1_hid, L0_gnn_W2_hid, L0_gnn_b2_hid, L0_gnn_W1_out, L0_gnn_b1_out, L0_gnn_W2_out, L0_gnn_b2_out), axis=-1)
    x = _layernorm(x + _L1_gnn_ref(x, L1_gnn_att, edge_weight, src, dst), axis=-1)
    return x

_drawn_inputs = setup_inputs


def setup_inputs(seed=0):
    import zlib

    import numpy as np

    out = dict(_drawn_inputs(seed))
    spreads = {'L0_gnn_b1_in': (0.0, 0.1),
     'L0_gnn_b2_in': (0.0, 0.1),
     'L0_gnn_b1_hid': (0.0, 0.1),
     'L0_gnn_b2_hid': (0.0, 0.1),
     'L0_gnn_b1_out': (0.0, 0.1),
     'L0_gnn_b2_out': (0.0, 0.1)}
    factors = {'edge_weight': 64.0, 'L1_gnn_att': 29.247}
    for name, (base, spread) in spreads.items():
        noise = np.random.default_rng([zlib.crc32(name.encode()), seed]).standard_normal(out[name].shape)
        drawn = base * np.exp(spread * noise) if base else spread * noise
        out[name] = jnp.asarray(drawn.astype(out[name].dtype))
    for name, factor in factors.items():
        out[name] = (out[name] * factor).astype(out[name].dtype)
    return out
```

```python
from contextlib import ExitStack

import concourse.bass as bass
from concourse import mybir

F32, BF16, I32 = mybir.dt.float32, mybir.dt.bfloat16, mybir.dt.int32
ALU = mybir.AluOpType
ACT = mybir.ActivationFunctionType
AX = mybir.AxisListType

P = 128
D = 128
N_NODES, N_EDGES = 6250, 206250
GROUP = P
TILE = 512
GPT = TILE // GROUP
N_TILES = -(-N_EDGES // TILE)
N_GROUPS = N_TILES * GPT
E_PAD = N_TILES * TILE
N_BLOCKS = -(-N_NODES // P)
N_PAD = N_BLOCKS * P
FULL_BLOCKS = N_NODES // P
TAIL_NODES = N_NODES - FULL_BLOCKS * P
PARTS = 3
BLOCK_COLS = PARTS * D
ROW_GROUPS = 13
ROW_PARTS = N_GROUPS // ROW_GROUPS
CHUNK = 4
N_CHUNKS = -(-N_TILES // CHUNK)
LAYERS = 3
SIDE = 8
EPS = 1e-5
SLOPE = 0.2
BIG = 3.2e38
ACCS = 4
ACC_ROWS = N_PAD + P
FLUSH = 32
FIN = 7
assert ROW_PARTS * ROW_GROUPS == N_GROUPS and ROW_PARTS <= P and N_BLOCKS % FIN == 0


def build(nc, x, src_cols, ew_cols, dst_line, dst_before_line, src_line, group_heads, tile_heads,
          w1, w2, b1, b2, att, out):
    ctx = ExitStack()
    with ctx:
        def sb(name, shape, dt=F32):
            return ctx.enter_context(nc.sbuf_tensor(name, shape, dt))

        def sem(name):
            return ctx.enter_context(nc.semaphore(name))

        def dram(name, shape, dt=F32):
            return nc.dram_tensor(name, shape, dt, kind="Internal").ap()

        b_table = dram("b_table", [N_PAD, D])
        prefix_max = dram("prefix_max", [E_PAD, D])
        rel_line = dram("rel_line", [ROW_PARTS, ROW_GROUPS * GROUP], BF16)
        cap_line = dram("cap_line", [ROW_PARTS, ROW_GROUPS * GROUP], BF16)
        lo_line = dram("lo_line", [ROW_PARTS, ROW_GROUPS * GROUP], BF16)
        hi_line = dram("hi_line", [ROW_PARTS, ROW_GROUPS * GROUP], BF16)
        acc = [dram(f"acc{i}", [ACC_ROWS, D]) for i in range(ACCS)]

        def line(t):
            return t.rearrange("q n -> (q n)")

        src_i = sb("src_i", [P, N_GROUPS], I32)
        x_nodes = sb("x_nodes", [P, N_BLOCKS, D])
        h_nodes = sb("h_nodes", [P, N_BLOCKS, D])
        parts = sb("parts", [P, (N_BLOCKS + 1) * BLOCK_COLS], BF16)
        group_block = sb("group_block", [1, N_GROUPS], I32)
        ident = sb("ident", [P, P])
        strict_lower = sb("strict_lower", [P, P])
        part_id = sb("part_id", [P, 2])
        part_id_i = sb("part_id_i", [P, 2], I32)
        node_id = sb("node_id", [P, N_BLOCKS])
        node_id_i = sb("node_id_i", [P, N_BLOCKS], I32)
        last_edge = sb("last_edge", [P, N_BLOCKS], I32)
        last_edge_f = sb("last_edge_f", [P, N_BLOCKS])
        has_edge = sb("has_edge", [P, N_BLOCKS])
        row_of_node = sb("row_of_node", [P, N_BLOCKS], I32)
        row_count = sb("row_count", [P, N_BLOCKS])
        in_row = sb("in_row", [P, N_BLOCKS])
        ones_row = sb("ones_row", [1, P], BF16)
        w_in = sb("w_in", [P, LAYERS, 2, D])
        w_node = sb("w_node", [P, LAYERS, 2, D])
        w_out = sb("w_out", [P, LAYERS, D])
        b1_all = sb("b1_all", [P, LAYERS, D])
        b2_all = sb("b2_all", [P, LAYERS, D])
        att_all = sb("att_all", [P, 2, D])
        rel_row = sb("rel_row", [1, 2, CHUNK * TILE], BF16)
        cap_all = sb("cap_all", [P, 2, CHUNK * TILE], BF16)
        b_rows = sb("b_rows", [P, 4, GPT, D])
        onehot = sb("onehot", [P, 2, 2, TILE], BF16)
        z_relu = sb("z_relu", [P, 2, TILE])
        running = sb("running", [P, 3, TILE])
        run_rows = sb("run_rows", [P, 3, TILE])
        node_x = sb("node_x", [P, 4, D])
        node_v = sb("node_v", [P, 2, D])
        node_xT = sb("node_xT", [P, 2, P])
        node_a = sb("node_a", [P, 2, D])
        node_r = sb("node_r", [P, 2, D])
        node_b = sb("node_b", [P, 4, D])
        src_f = sb("src_f", [P, N_GROUPS])
        coef = sb("coef", [P, N_GROUPS])
        score = sb("score", [P, N_GROUPS])
        s_node = sb("s_node", [P, N_BLOCKS])
        t_node = sb("t_node", [P, N_BLOCKS])
        tmp_node = sb("tmp_node", [P, 2, N_BLOCKS])
        s_parts = sb("s_parts", [P, PARTS, N_BLOCKS], BF16)
        t_parts = sb("t_parts", [P, (N_BLOCKS + 1) * PARTS], BF16)
        hilo_row = cap_all[0:2, :, :]
        sel_lo = sb("sel_lo", [2, P], BF16)
        sel_hi = sb("sel_hi", [2, P], BF16)
        sel_src = sb("sel_src", [2, P], BF16)
        sel_src_f = sb("sel_src_f", [2, 3, P])
        lo_onehot = sb("lo_onehot", [P, 2, TILE], BF16)
        s_picked = run_rows[0:N_BLOCKS, 0:2, :]
        s_masked = running[0:N_BLOCKS, 0:2, :]
        ones_col = sb("ones_col", [P, 1])
        stats = sb("stats", [P, 6])
        mv = sb("mv", [P, 2])
        rstd = sb("rstd", [P, 2])
        pad_cap = sb("pad_cap", [P, 1])
        soft = sb("soft", [P, 6])
        dup_scratch = sb("dup_scratch", [P, GPT, P], BF16)
        dup_count = sb("dup_count", [P, 2, GPT])
        dup_pick = sb("dup_pick", [P, GPT])
        scatter_row = sb("scatter_row", [P, 4, GPT], I32)

        ps_bc = [ctx.enter_context(nc.psum_tensor(f"ps_bc{i}", [P, TILE], F32)) for i in range(2)]
        ps_z = [ctx.enter_context(nc.psum_tensor(f"ps_z{i}", [P, TILE], F32)) for i in range(2)]
        ps_h = [ctx.enter_context(nc.psum_tensor(f"ps_h{i}", [P, TILE], F32)) for i in range(2)]
        ps_t = [ctx.enter_context(nc.psum_tensor(f"ps_t{i}", [P, TILE], F32)) for i in range(2)]

        same_src = z_relu[:, :, :].rearrange("p r (g e) -> p r g e", g=GPT)

        s_in = sem("s_in")
        s_const = sem("s_const")
        s_prep = sem("s_prep")
        s_line = sem("s_line")
        s_x = sem("s_x")
        s_ready = sem("s_ready")
        s_chunk = [sem(f"s_chunk{i}") for i in range(2)]
        s_bc = sem("s_bc")
        s_oh = sem("s_oh")
        s_g = [sem(f"s_g{i}") for i in range(4)]
        s_z = sem("s_z")
        s_relu = sem("s_relu")
        s_h = sem("s_h")
        s_scan = sem("s_scan")
        s_tr = sem("s_tr")
        s_rr = sem("s_rr")
        s_st = [sem(f"s_st{i}") for i in range(3)]
        s_rowg = [sem(f"s_rowg{i}") for i in range(2)]
        s_rowd = sem("s_rowd")
        s_rowi = sem("s_rowi")
        s_ends = sem("s_ends")
        s_nx = [sem(f"s_nx{i}") for i in range(4)]
        s_nv = sem("s_nv")
        s_nt = sem("s_nt")
        s_nc = sem("s_nc")
        s_nab = sem("s_nab")
        s_nf = sem("s_nf")
        s_nb = sem("s_nb")
        s_nst = [sem(f"s_nst{i}") for i in range(4)]
        s_dve = sem("s_dve")
        s_hn = sem("s_hn")
        s_sq = sem("s_sq")
        s_lo = sem("s_lo")
        s_loh = sem("s_loh")
        s_pick = sem("s_pick")
        s_pickc = sem("s_pickc")
        s_hi = sem("s_hi")
        s_msk = sem("s_msk")
        s_sc = sem("s_sc")
        s_fl = sem("s_fl")
        s_red = sem("s_red")
        s_all = sem("s_all")
        s_exp = sem("s_exp")
        s_coef = sem("s_coef")
        s_hl = [sem(f"s_hl{i}") for i in range(2)]
        s_zero = sem("s_zero")
        s_hx = sem("s_hx")
        s_hxc = sem("s_hxc")
        s_same = sem("s_same")
        s_idx = sem("s_idx")
        s_ms = sem("s_ms")
        s_msc = sem("s_msc")
        s_acc = [sem(f"s_acc{i}") for i in range(ACCS)]
        s_fin = [sem(f"s_fin{i}") for i in range(2)]
        s_fd = sem("s_fd")
        s_out = [sem(f"s_out{i}") for i in range(2)]

        N_IN = 16 * (7 + 5 * LAYERS)

        prep = h_nodes[:, :, :].rearrange("p b d -> p (b d)")
        L = ROW_GROUPS * GROUP
        prep_i = prep.bitcast(I32)
        dst_now = prep_i[0:ROW_PARTS, 0:L]
        dst_before = prep_i[0:ROW_PARTS, L:2 * L]
        src_now = prep_i[0:ROW_PARTS, 2 * L:3 * L]
        rel_sb = parts[0:ROW_PARTS, 0:L]
        cap_sb = parts[0:ROW_PARTS, L:2 * L]
        lo_sb = parts[0:ROW_PARTS, 2 * L:3 * L]
        hi_sb = parts[0:ROW_PARTS, 3 * L:4 * L]
        lo_i = parts[0:ROW_PARTS, 4 * L:6 * L].bitcast(I32)
        hi_i = parts[0:ROW_PARTS, 6 * L:8 * L].bitcast(I32)
        base_i = parts[0:ROW_PARTS, 8 * L:8 * L + 2 * ROW_GROUPS].bitcast(I32)
        eq_f = parts[0:ROW_PARTS, 9 * L:11 * L].bitcast(F32)
        row_dst = sb("row_dst", [P, 2, TILE], I32)
        row_junk = sb("row_junk", [P, TILE], BF16)
        dst_tiles = dst_line.rearrange("(t e) -> t e", e=TILE)
        heads_i = score[:, 0:N_TILES].bitcast(I32)
        heads_f = score[:, N_TILES:2 * N_TILES]

        def gathered(l, i):
            return 16 * ((l * N_BLOCKS + 3 - i) // 4)

        def acc_count(a, n):
            return 16 * ((n + ACCS - 1 - a) // ACCS)

        def acc_in(slot, a):
            o = (slot * ACCS + a) * FIN * D
            return parts[:, :].bitcast(F32)[:, o:o + FIN * D].rearrange("p (b d) -> p b d", d=D)

        def chunk_count(C):
            edge = LAYERS * N_CHUNKS
            uses = [c for c in range(C % 2, C + 1, 2)]
            return sum(32 if c < edge else 16 for c in uses)

        block = ctx.enter_context(nc.Block())

        def tiles_in(c):
            return min(CHUNK, N_TILES - c * CHUNK)

        def store_out(sp, k):
            sp.wait_ge(s_fd, k + 1)
            b0 = k * FIN
            full = min(FIN, FULL_BLOCKS - b0)
            sp.dma_start(out[b0 * P:(b0 + full) * P, :].rearrange("(b p) d -> p b d", p=P),
                         h_nodes[:, b0:b0 + full, :]).then_inc(s_out[k % 2], 16)
            if full < FIN:
                sp.dma_start(out[FULL_BLOCKS * P:N_NODES, :],
                             h_nodes[0:TAIL_NODES, FULL_BLOCKS, :]).then_inc(s_out[k % 2], 16)

        @block.sync
        def _(sp):
            def as_rows(t):
                return t.rearrange("(q n) -> q n", q=ROW_PARTS)

            sp.dma_start(dst_now, as_rows(dst_line)).then_inc(s_in, 16)
            sp.dma_start(dst_before, as_rows(dst_before_line)).then_inc(s_in, 16)
            sp.dma_start(src_now, as_rows(src_line)).then_inc(s_in, 16)
            sp.dma_start(group_block[:, :], group_heads.rearrange("(a n) -> a n", a=1)).then_inc(s_in, 16)
            sp.dma_start(heads_i[:, :], tile_heads.rearrange("(a n) -> a n", a=1).to_broadcast([P, N_TILES])).then_inc(s_in, 16)
            sp.dma_start(src_i[:, :], src_cols).then_inc(s_in, 16)
            sp.dma_start(coef[:, :], ew_cols).then_inc(s_in, 16)
            for l in range(LAYERS):
                sp.dma_start(w_in[:, l, 0, :], w1[l][0:D, :]).then_inc(s_in, 16)
                sp.dma_start(w_in[:, l, 1, :], w1[l][D:2 * D, :]).then_inc(s_in, 16)
                sp.dma_start(w_out[:, l, :], w2[l]).then_inc(s_in, 16)
                sp.dma_start(b1_all[:, l, :], b1[l].rearrange("(a n) -> a n", a=1).to_broadcast([P, D])).then_inc(s_in, 16)
                sp.dma_start(b2_all[:, l, :], b2[l].rearrange("(a n) -> a n", a=1).to_broadcast([P, D])).then_inc(s_in, 16)
            for i in range(2):
                sp.dma_start(att_all[:, i, :], att[i * D:(i + 1) * D, :].rearrange("n a -> a n").to_broadcast([P, D])).then_inc(s_x, 16)
            sp.wait_ge(s_const, 1)
            sp.dma_start(x_nodes[:, 0:FULL_BLOCKS, :],
                         x[0:FULL_BLOCKS * P, :].rearrange("(b p) d -> p b d", p=P)).then_inc(s_x, 16)
            sp.dma_start(x_nodes[0:TAIL_NODES, FULL_BLOCKS, :], x[FULL_BLOCKS * P:N_NODES, :]).then_inc(s_x, 16)
            sp.wait_ge(s_prep, 1)
            for dst_t, s in ((rel_line, rel_sb), (cap_line, cap_sb), (lo_line, lo_sb), (hi_line, hi_sb)):
                sp.dma_start(dst_t, s).then_inc(s_line, 16)
            sp.wait_ge(s_line, 64)
            for a in range(ACCS):
                for b0 in range(0, N_BLOCKS + 1, GPT):
                    nb = min(GPT, N_BLOCKS + 1 - b0)
                    sp.dma_start(acc[a][b0 * P:(b0 + nb) * P, :].rearrange("(b p) d -> p b d", p=P),
                                   run_rows[:, 0, 0:nb * D].rearrange("p (b d) -> p b d", d=D)).then_inc(s_zero, 16)

            def load_chunk(c_all, c, with_cap):
                e0, n = c * CHUNK * TILE, tiles_in(c) * TILE
                slot = c_all % 2
                sp.dma_start(rel_row[:, slot, 0:n],
                             line(rel_line)[e0:e0 + n].rearrange("(a n) -> a n", a=1)).then_inc(s_chunk[slot], 16)
                if with_cap:
                    sp.dma_start(cap_all[:, slot, 0:n],
                                 line(cap_line)[e0:e0 + n].rearrange("(a n) -> a n", a=1).to_broadcast([P, n])).then_inc(s_chunk[slot], 16)
                else:
                    for r, t in enumerate((hi_line, lo_line)):
                        sp.dma_start(hilo_row[r:r + 1, slot, 0:n],
                                     line(t)[e0:e0 + n].rearrange("(a n) -> a n", a=1)).then_inc(s_hl[slot], 16)

            def store_b(l, k):
                n = l * N_BLOCKS + k
                sp.wait_ge(s_nb, n + 1)
                if l and not k:
                    sp.wait_ge(s_z, l * N_TILES)
                sp.dma_start(b_table[k * P:(k + 1) * P, :], node_b[:, n % 4, :]).then_inc(s_nst[n % 4], 16)

            for l in range(LAYERS):
                for k in range(N_BLOCKS):
                    store_b(l, k)
                if l:
                    for i in range(4):
                        sp.wait_ge(s_nx[i], gathered(l, i))
                load_chunk(l * N_CHUNKS, 0, True) if l == 0 else None
                for t in range(N_TILES):
                    T = l * N_TILES + t
                    if t % CHUNK == 0:
                        c = t // CHUNK
                        C = l * N_CHUNKS + c
                        if C + 1 < LAYERS * N_CHUNKS:
                            nl, ncx = divmod(C + 1, N_CHUNKS)
                            if C >= 1:
                                sp.wait_ge(s_bc, T)
                                sp.wait_ge(s_scan, T)
                            load_chunk(C + 1, ncx, True)
                    sp.wait_ge(s_rr, T + 1)
                    sp.dma_start(prefix_max[t * TILE:(t + 1) * TILE, :].rearrange("(g e) d -> e g d", g=GPT),
                                 run_rows[:, T % 3, :].rearrange("p (g d) -> p g d", g=GPT)).then_inc(s_st[T % 3], 16)

            for ph in range(2):
                for c in range(N_CHUNKS):
                    C = (LAYERS + ph) * N_CHUNKS + c
                    q = ph * N_CHUNKS + c
                    T0 = (LAYERS + ph) * N_TILES
                    if q >= 2:
                        pq, pc = divmod(q - 2, N_CHUNKS)
                        done = pq * N_TILES + min((pc + 1) * CHUNK, N_TILES)
                        sp.wait_ge(s_bc, LAYERS * N_TILES + done)
                        sp.wait_ge(s_hi, done)
                    elif q == 0:
                        sp.wait_ge(s_bc, LAYERS * N_TILES)
                        sp.wait_ge(s_scan, LAYERS * N_TILES)
                    load_chunk(C, c, False)

            for i in range(ACCS):
                sp.wait_ge(s_acc[i], acc_count(i, N_GROUPS))
            for k in range(N_BLOCKS // FIN):
                if k >= 2:
                    sp.wait_ge(s_fd, k - 1)
                for i in range(ACCS):
                    sp.dma_start(acc_in(k % 2, i),
                                 acc[i][k * FIN * P:(k + 1) * FIN * P, :].rearrange("(b p) d -> p b d", p=P)).then_inc(s_fin[k % 2], 16)
                if k >= 1:
                    store_out(sp, k - 1)
            store_out(sp, N_BLOCKS // FIN - 1)
            for i in range(2):
                n_full = (N_BLOCKS // FIN + 1 - i) // 2
                extra = 1 if (N_BLOCKS // FIN - 1) % 2 == i else 0
                sp.wait_ge(s_out[i], 16 * (n_full + extra))

        @block.gpsimd
        def _(pool):
            pool.memset(x_nodes[:, FULL_BLOCKS, :], 0.0).then_inc(s_const, 1)
            pool.memset(ident[:, :], 0.0)
            pool.memset(strict_lower[:, :], 1.0)
            pool.memset(ones_row[:, :], 1.0)
            pool.memset(ones_col[:, :], 1.0)
            pool.memset(run_rows[:, 0, :], 0.0)
            pool.memset(sel_src_f[:, :, :], 0.0).then_inc(s_const, 1)
            pool.wait_ge(s_const, 2)
            pool.affine_select(out=ident[:, :], in_=ident[:, :], compare_op=ALU.not_equal, fill=1.0,
                               base=0, pattern=[[-1, P]], channel_multiplier=1)
            pool.affine_select(out=strict_lower[:, :], in_=strict_lower[:, :], compare_op=ALU.is_gt, fill=0.0,
                               base=0, pattern=[[-1, P]], channel_multiplier=1)
            for j, (row, val) in enumerate(((1, 1.0), (0, 1.0), (1, 1.0))):
                pool.affine_select(out=sel_src_f[:, j, :], in_=sel_src_f[:, j, :], compare_op=ALU.not_equal, fill=val,
                                   base=-row, pattern=[[0, P]], channel_multiplier=1)
            pool.iota(part_id_i[:, :], pattern=[[P, 2]], base=0, channel_multiplier=1)
            pool.iota(node_id_i[:, :], pattern=[[P, N_BLOCKS]], base=0, channel_multiplier=1).then_inc(s_const, 1)
            pool.wait_ge(s_const, 3)
            pool.affine_select(out=sel_src_f[:, 2, :], in_=sel_src_f[:, 2, :], compare_op=ALU.not_equal, fill=float(P),
                               base=0, pattern=[[0, P]], channel_multiplier=1).then_inc(s_const, 1)
            def row_gather(k):
                pool.wait_ge(s_rowi, 1)
                if k >= 2:
                    pool.wait_ge(s_rowd, k - 1)
                pool.indirect_dma_start(out=row_dst[:, k % 2, :], out_offset=None, in_=dst_tiles,
                                        in_offset=bass.IndirectOffsetOnAxis(ap=row_of_node[:, k:k + 1], axis=0)
                                        ).then_inc(s_rowg[k % 2], 16)

            def node_gather(l, k):
                n = (l - 1) * N_BLOCKS + k
                if n >= 4:
                    pool.wait_ge(s_nv, n - 3)
                pool.indirect_dma_start(out=node_x[:, n % 4, :], out_offset=None, in_=prefix_max,
                                        in_offset=bass.IndirectOffsetOnAxis(ap=last_edge[:, k:k + 1], axis=0)
                                        ).then_inc(s_nx[n % 4], 16)

            pool.wait_ge(s_in, N_IN)
            for l in range(LAYERS):
                for i in range(4):
                    pool.wait_ge(s_nst[i], 16 * (((l + 1) * N_BLOCKS + 3 - i) // 4))
                for t in range(N_TILES):
                    T = l * N_TILES + t
                    if T >= 4:
                        pool.wait_ge(s_z, T - 3)
                    for g in range(GPT):
                        i = t * GPT + g
                        pool.indirect_dma_start(out=b_rows[:, T % 4, g, :], out_offset=None, in_=b_table,
                                                in_offset=bass.IndirectOffsetOnAxis(ap=src_i[:, i:i + 1], axis=0)
                                                ).then_inc(s_g[T % 4], 16)
                    if l == 0 and t % SIDE == 3 and t // SIDE < N_BLOCKS:
                        row_gather(t // SIDE)
                for i in range(3):
                    pool.wait_ge(s_st[i], 16 * (((l + 1) * N_TILES + 2 - i) // 3))
                pool.wait_ge(s_ends, 1)
                for k in range(N_BLOCKS):
                    node_gather(l + 1, k)

            pool.wait_ge(s_red, 1)
            pool.partition_all_reduce(soft[:, 1:2], soft[:, 0:1], P, bass.bass_isa.ReduceOp.max).then_inc(s_all, 1)
            pool.wait_ge(s_exp, 1)
            pool.partition_all_reduce(soft[:, 4:5], soft[:, 3:4], P, bass.bass_isa.ReduceOp.add).then_inc(s_all, 1)
            pool.wait_ge(s_zero, 16 * ACCS * -(-(N_BLOCKS + 1) // GPT))
            for t in range(N_TILES):
                pool.wait_ge(s_idx, t + 1)
                pool.wait_ge(s_msc, t + 1)
                for g in range(GPT):
                    i = t * GPT + g
                    a = i % ACCS
                    if i >= ACCS:
                        pool.wait_ge(s_acc[a], acc_count(a, i))
                    pool.indirect_dma_start(out=acc[a],
                                            out_offset=bass.IndirectOffsetOnAxis(ap=scatter_row[:, t % 4, g:g + 1], axis=0),
                                            in_=b_rows[:, t % 4, g, :], in_offset=None,
                                            compute_op=ALU.add).then_inc(s_acc[a], 16)

        @block.tensor
        def _(pe):
            def broadcast_rel(T, t):
                C = T // N_TILES * N_CHUNKS + t // CHUNK
                if t % CHUNK == 0:
                    pe.wait_ge(s_chunk[C % 2], chunk_count(C))
                if T >= 2:
                    pe.wait_ge(s_oh, T - 1)
                o = (t % CHUNK) * TILE
                pe.matmul(ps_bc[T % 2][:, :], ones_row[:, :], rel_row[:, C % 2, o:o + TILE],
                          start=True, stop=True).then_inc(s_bc, 1)

            def window(i):
                return pe.value_load(group_block[0:1, i:i + 1], min_val=0, max_val=N_BLOCKS - 1)

            pe.wait_ge(s_const, 4)
            pe.wait_ge(s_ready, 1)
            pe.wait_ge(s_in, N_IN)
            for l in range(LAYERS):
                for k in range(N_BLOCKS + 1):
                    n = l * N_BLOCKS + k
                    if k < N_BLOCKS:
                        if l == 0:
                            pe.wait_ge(s_x, 64)
                            xin = x_nodes[:, k, :]
                        else:
                            m = n - N_BLOCKS
                            pe.wait_ge(s_nv, m + 1)
                            xin = node_v[:, m % 2, :]
                        if n >= 2:
                            pe.wait_ge(s_nc, n - 1)
                        pe.transpose(ps_z[n % 2][:, 0:P], xin, ident[:, :]).then_inc(s_nt, 1)
                    if k >= 1:
                        n -= 1
                        pe.wait_ge(s_nc, n + 1)
                        if n >= 2:
                            pe.wait_ge(s_nf, n - 1)
                            pe.wait_ge(s_nb, n - 1)
                        for bank, w in ((ps_h, 0), (ps_t, 1)):
                            last = pe.matmul(bank[n % 2][:, 0:D], node_xT[:, n % 2, :], w_node[:, l, w, :],
                                             start=True, stop=True)
                        last.then_inc(s_nab, 1)
                pe.wait_ge(s_nf, (l + 1) * N_BLOCKS)
                pe.wait_ge(s_nb, (l + 1) * N_BLOCKS)
                broadcast_rel(l * N_TILES, 0)
                for t in range(N_TILES + 2):
                    T = l * N_TILES + t
                    if t + 1 < N_TILES:
                        broadcast_rel(T + 1, t + 1)
                    if t < N_TILES:
                        regs = [window(t * GPT + g) for g in range(GPT)]
                        pe.wait_ge(s_oh, T + 1)
                        pe.wait_ge(s_g[T % 4], 16 * GPT * (T // 4 + 1))
                        if T >= 2:
                            pe.wait_ge(s_relu, T - 1)
                        for g in range(GPT):
                            z = ps_z[T % 2][:, g * GROUP:(g + 1) * GROUP]
                            pe.matmul(z, b_rows[:, T % 4, g, :], ident[:, :], start=True, stop=False)
                            for half in range(2):
                                for part in range(PARTS):
                                    last = pe.matmul(
                                        z, parts[:, bass.ds(regs[g] * BLOCK_COLS + (half * PARTS + part) * D, D)],
                                        onehot[:, T % 2, half, g * GROUP:(g + 1) * GROUP],
                                        start=False, stop=(half == 1 and part == PARTS - 1))
                        last.then_inc(s_z, 1)
                    if 1 <= t <= N_TILES:
                        u = T - 1
                        pe.wait_ge(s_relu, u + 1)
                        if u >= 2:
                            pe.wait_ge(s_scan, u - 1)
                        pe.matmul(ps_h[u % 2][:, :], w_out[:, l, :], z_relu[:, u % 2, :],
                                  start=True, stop=True).then_inc(s_h, 1)
                    if 2 <= t:
                        u = T - 2
                        pe.wait_ge(s_scan, u + 1)
                        if u >= 2:
                            pe.wait_ge(s_rr, u - 1)
                        for g in range(GPT):
                            last = pe.transpose(ps_t[u % 2][:, g * GROUP:(g + 1) * GROUP],
                                                running[:, u % 3, g * GROUP:(g + 1) * GROUP], ident[:, :])
                        last.then_inc(s_tr, 1)

            T0 = LAYERS * N_TILES
            pe.wait_ge(s_hn, N_BLOCKS + 1)

            def hl_wait(q, t):
                if t % CHUNK == 0:
                    pe.wait_ge(s_hl[(LAYERS * N_CHUNKS + q) % 2], 32 * (q // 2 + 1))

            for t in range(N_TILES + 2):
                c = t // CHUNK
                o = (t % CHUNK) * TILE
                if t < N_TILES:
                    broadcast_rel(T0 + t, t)
                    hl_wait(c, t)
                    if t >= 1:
                        pe.wait_ge(s_loh, t)
                    pe.matmul(ps_z[0][:, :], sel_lo[:, :], hilo_row[:, (LAYERS * N_CHUNKS + c) % 2, o:o + TILE],
                              start=True, stop=True).then_inc(s_lo, 1)
                if 1 <= t <= N_TILES:
                    u = t - 1
                    uc, uo = u // CHUNK, (u % CHUNK) * TILE
                    pe.wait_ge(s_loh, u + 1)
                    if u >= 2:
                        pe.wait_ge(s_pickc, u - 1)
                    for part in range(PARTS):
                        last = pe.matmul(ps_h[u % 2][0:N_BLOCKS, :], s_parts[:, part, :], lo_onehot[:, u % 2, :],
                                         start=(part == 0), stop=(part == PARTS - 1))
                    last.then_inc(s_pick, 1)
                    if u >= 1:
                        pe.wait_ge(s_msk, u)
                    pe.matmul(ps_z[1][0:N_BLOCKS, :], sel_hi[:, 0:N_BLOCKS],
                              hilo_row[:, (LAYERS * N_CHUNKS + uc) % 2, uo:uo + TILE],
                              start=True, stop=True).then_inc(s_hi, 1)
                if t >= 2:
                    u = t - 2
                    fb = u // FLUSH
                    if u % FLUSH == 0 and fb >= 2:
                        pe.wait_ge(s_fl, fb - 1)
                    pe.wait_ge(s_oh, T0 + u + 1)
                    pe.wait_ge(s_msk, u + 1)
                    for g in range(GPT):
                        i = u * GPT + g
                        col = (i % (FLUSH * GPT)) * 4
                        w = window(i)
                        es = slice(g * GROUP, (g + 1) * GROUP)
                        for half in range(2):
                            pe.matmul(ps_t[fb % 2][:, col:col + PARTS], onehot[:, (T0 + u) % 2, half, es],
                                      t_parts[:, bass.ds(w * PARTS + half * PARTS, PARTS)],
                                      start=(half == 0), stop=(half == 1))
                        last = pe.matmul(ps_t[fb % 2][:, col + PARTS:col + 4], s_masked[:, u % 2, es],
                                         ones_col[0:N_BLOCKS, :], start=True, stop=True)
                    last.then_inc(s_sc, 1)

            T1 = T0 + N_TILES
            pe.wait_ge(s_fl, -(-N_TILES // FLUSH))
            for t in range(N_TILES + 2):
                c = t // CHUNK
                o = (t % CHUNK) * TILE
                if t < N_TILES:
                    broadcast_rel(T1 + t, t)
                    hl_wait(N_CHUNKS + c, t)
                    if t >= 2:
                        pe.wait_ge(s_same, t - 1)
                    pe.matmul(ps_t[t % 2][:, :], sel_src[:, :], hilo_row[:, ((LAYERS + 1) * N_CHUNKS + c) % 2, o:o + TILE],
                              start=True, stop=True).then_inc(s_hi, 1)
                if 1 <= t <= N_TILES:
                    u = t - 1
                    pe.wait_ge(s_oh, T1 + u + 1)
                    if u >= 2:
                        pe.wait_ge(s_hxc, u - 1)
                    for g in range(GPT):
                        w = window(u * GPT + g)
                        for half in range(2):
                            for part in range(PARTS):
                                last = pe.matmul(ps_z[u % 2][:, g * D:(g + 1) * D],
                                                 onehot[:, (T1 + u) % 2, half, g * GROUP:(g + 1) * GROUP],
                                                 parts[:, bass.ds(w * BLOCK_COLS + (half * PARTS + part) * D, D)],
                                                 start=(half == 0 and part == 0), stop=(half == 1 and part == PARTS - 1))
                    last.then_inc(s_hx, 1)
                if t >= 2:
                    u = t - 2
                    pe.wait_ge(s_hxc, u + 1)
                    pe.wait_ge(s_same, u + 1)
                    if u >= 2:
                        pe.wait_ge(s_msc, u - 1)
                    for g in range(GPT):
                        last = pe.matmul(ps_h[u % 2][:, g * D:(g + 1) * D], same_src[:, u % 2, g, :],
                                         running[:, u % 2, g * D:(g + 1) * D], start=True, stop=True)
                    last.then_inc(s_ms, 1)

        @block.scalar
        def _(act):
            for l in range(LAYERS):
                for k in range(N_BLOCKS + 1):
                    n = l * N_BLOCKS + k
                    if k < N_BLOCKS:
                        act.wait_ge(s_nt, n + 1)
                        if n >= 2:
                            act.wait_ge(s_nab, n - 1)
                        act.activation(node_xT[:, n % 2, :], ps_z[n % 2][:, 0:P], ACT.Copy).then_inc(s_nc, 1)
                    if k >= 1:
                        n -= 1
                        act.wait_ge(s_nab, n + 1)
                        if n >= 4:
                            act.wait_ge(s_nst[n % 4], 16 * (n // 4))
                        act.activation(node_b[:, n % 4, :], ps_t[n % 2][:, 0:D], ACT.Copy).then_inc(s_nb, 1)
                for t in range(N_TILES + 2):
                    T = l * N_TILES + t
                    if t < N_TILES:
                        act.wait_ge(s_z, T + 1)
                        if T >= 2:
                            act.wait_ge(s_h, T - 1)
                        act.activation(z_relu[:, T % 2, :], ps_z[T % 2][:, :], ACT.Relu).then_inc(s_relu, 1)
                    if t >= 2:
                        u = T - 2
                        act.wait_ge(s_tr, u + 1)
                        if u >= 3:
                            act.wait_ge(s_st[u % 3], 16 * (u // 3))
                        if u == 0:
                            act.wait_ge(s_zero, 16 * ACCS * -(-(N_BLOCKS + 1) // GPT))
                        act.activation(run_rows[:, u % 3, :], ps_t[u % 2][:, :], ACT.Copy).then_inc(s_rr, 1)
            for k in range(N_BLOCKS):
                act.wait_ge(s_sq, 2 * k + 1)
                act.activation(rstd[:, 0:1], mv[:, 1:2], ACT.Sqrt).then_inc(s_sq, 1)
            for t in range(N_TILES):
                act.wait_ge(s_pick, t + 1)
                if t >= 2:
                    act.wait_ge(s_msk, t - 1)
                act.activation(s_picked[:, t % 2, :], ps_h[t % 2][0:N_BLOCKS, :], ACT.Copy).then_inc(s_pickc, 1)
            act.wait_ge(s_red, 2)
            act.activation(score[:, :], score[:, :], ACT.Exp, bias=soft[:, 2:3], scale=1.0,
                           accum_out=soft[:, 3:4]).then_inc(s_exp, 1)
            for t in range(N_TILES + 1):
                if t < N_TILES:
                    act.wait_ge(s_hx, t + 1)
                    if t >= 2:
                        act.wait_ge(s_ms, t - 1)
                    act.activation(running[:, t % 2, :], ps_z[t % 2][:, :], ACT.Copy).then_inc(s_hxc, 1)
                if t >= 1:
                    u = t - 1
                    act.wait_ge(s_ms, u + 1)
                    if u >= 4:
                        for a in range(ACCS):
                            act.wait_ge(s_acc[a], acc_count(a, (u - 3) * GPT))
                    act.activation(b_rows[:, u % 4, :, :].rearrange("p g d -> p (g d)"), ps_h[u % 2][:, :],
                                   ACT.Copy).then_inc(s_msc, 1)
            for k in range(N_BLOCKS):
                act.wait_ge(s_sq, 2 * (N_BLOCKS + k) + 1)
                act.activation(rstd[:, 0:1], mv[:, 1:2], ACT.Sqrt).then_inc(s_sq, 1)

        @block.vector
        def _(dve):
            chained = [0]

            def link(ins):
                chained[0] += 1
                ins.then_inc(s_dve, 1)
                dve.wait_ge(s_dve, chained[0])

            dve.wait_ge(s_in, N_IN)
            dve.wait_ge(s_const, 4)
            g3 = lambda t: t.rearrange("q (g e) -> q g e", e=GROUP)
            link(dve.tensor_scalar(base_i, g3(dst_now)[:, :, 0], 7, 7, ALU.logical_shift_right, ALU.logical_shift_left))
            dve.tensor_tensor(g3(rel_sb), g3(dst_now),
                              base_i.rearrange("q (g a) -> q g a", a=1).to_broadcast([ROW_PARTS, ROW_GROUPS, GROUP]), ALU.subtract)
            dve.tensor_scalar(lo_i, src_now, P - 1, None, ALU.bitwise_and)
            dve.tensor_scalar(hi_i, src_now, 7, None, ALU.logical_shift_right)
            link(dve.tensor_tensor(eq_f, dst_now, dst_before, ALU.is_equal))
            link(dve.tensor_scalar(eq_f, eq_f, 2.0, -1.0, ALU.mult, ALU.add))
            dve.tensor_scalar(cap_sb, eq_f, BIG, None, ALU.mult)
            dve.tensor_copy(lo_sb, lo_i)
            dve.tensor_copy(hi_sb, hi_i).then_inc(s_prep, 1)
            dve.tensor_copy(part_id[:, :], part_id_i[:, :])
            dve.tensor_copy(node_id[:, :], node_id_i[:, :])
            dve.tensor_copy(src_f[:, :], src_i[:, :])
            dve.tensor_copy(sel_lo[:, :], sel_src_f[:, 0, :])
            dve.tensor_copy(sel_hi[:, :], sel_src_f[:, 1, :])
            dve.tensor_copy(sel_src[:, :], sel_src_f[:, 2, :])
            dve.tensor_scalar(group_block[:, :], group_block[:, :], 7, None, ALU.logical_shift_right)
            for l in range(LAYERS):
                dve.tensor_tensor(w_node[:, l, 0, :], w_in[:, l, 0, :], w_in[:, l, 1, :], ALU.subtract)
                dve.tensor_copy(w_node[:, l, 1, :], w_in[:, l, 1, :])
            dve.wait_ge(s_line, 64)
            dve.memset(t_parts[:, N_BLOCKS * PARTS:], 0.0)
            link(dve.memset(parts[:, N_BLOCKS * BLOCK_COLS:], 0.0))
            link(dve.tensor_copy(heads_f[:, :], heads_i[:, :]))
            for k in range(N_BLOCKS):
                link(dve.tensor_scalar(row_junk[:, 0:N_TILES], heads_f[:, :], node_id[:, k:k + 1], 0.0,
                                       ALU.is_le, ALU.add, accum_out=row_count[:, k:k + 1]))
            link(dve.tensor_scalar(row_count[:, :], row_count[:, :], -1.0, 0.0, ALU.add, ALU.max))
            dve.tensor_copy(row_of_node[:, :], row_count[:, :]).then_inc(s_rowi, 1)
            dve.tensor_copy(soft[:, 0:1], part_id[:, 0:1]).then_inc(s_ready, 1)

            def onehots(T):
                dve.wait_ge(s_bc, T + 1)
                if T >= 2:
                    free_onehot(T)
                dve.tensor_scalar(onehot[:, T % 2, 0, :], ps_bc[T % 2][:, :], part_id[:, 0:1], None, ALU.is_equal)
                dve.tensor_scalar(onehot[:, T % 2, 1, :], ps_bc[T % 2][:, :], part_id[:, 1:2], None,
                                  ALU.is_equal).then_inc(s_oh, 1)

            def free_onehot(T):
                u = T - 2
                ph, _ = divmod(u, N_TILES)
                if ph < LAYERS:
                    dve.wait_ge(s_z, u + 1)
                elif ph == LAYERS:
                    dve.wait_ge(s_sc, u + 1 - LAYERS * N_TILES)
                else:
                    dve.wait_ge(s_hx, u + 1 - (LAYERS + 1) * N_TILES)

            def split(dst3, val, rest, link_first=True):
                link(dve.tensor_copy(dst3[0], val))
                link(dve.tensor_tensor(rest, val, dst3[0], ALU.subtract))
                link(dve.tensor_copy(dst3[1], rest))
                return dve.tensor_tensor(dst3[2], rest, dst3[1], ALU.subtract)

            def block_parts(k):
                return [parts[:, k * BLOCK_COLS + j * D:k * BLOCK_COLS + (j + 1) * D] for j in range(PARTS)]

            def aggregate(l, k):
                m = (l - 1) * N_BLOCKS + k
                dve.wait_ge(s_nx[m % 4], 16 * (m // 4 + 1))
                link(dve.tensor_tensor(node_x[:, m % 4, :], node_x[:, m % 4, :], b2_all[:, l - 1, :], ALU.add))
                if l < LAYERS:
                    if m >= 2:
                        dve.wait_ge(s_nt, N_BLOCKS + m - 1)
                    dve.tensor_scalar(node_v[:, m % 2, :], node_x[:, m % 4, :], has_edge[:, k:k + 1], 0.0,
                                      ALU.mult, ALU.max).then_inc(s_nv, 1)
                else:
                    link(dve.tensor_scalar(node_r[:, 1, :], node_x[:, m % 4, :], has_edge[:, k:k + 1], None, ALU.mult))
                    link(dve.tensor_tensor(node_a[:, 0, :], node_r[:, 1, :], x_nodes[:, k, :], ALU.add))

            sq = [0]

            def layernorm(dst, val):
                link(dve.bn_stats(stats[:, :], val))
                link(dve.bn_aggr(mv[:, :], stats[:, :]))
                dve.tensor_scalar(mv[:, 1:2], mv[:, 1:2], EPS, None, ALU.add).then_inc(s_sq, 1)
                sq[0] += 2
                dve.wait_ge(s_sq, sq[0])
                link(dve.reciprocal(rstd[:, 1:2], rstd[:, 0:1]))
                return dve.tensor_scalar(dst, val, mv[:, 0:1], rstd[:, 1:2], ALU.subtract, ALU.mult)

            def node_stage(l):
                for k in range(N_BLOCKS):
                    n = l * N_BLOCKS + k
                    if l:
                        aggregate(l, k)
                    if k >= 1:
                        finish_a(l, k - 1)
                finish_a(l, N_BLOCKS - 1)

            def finish_a(l, k):
                n = l * N_BLOCKS + k
                dve.wait_ge(s_nab, n + 1)
                link(dve.tensor_tensor(node_a[:, n % 2, :], ps_h[n % 2][:, 0:D], b1_all[:, l, :], ALU.add))
                if l and k == 0:
                    dve.wait_ge(s_z, l * N_TILES)
                split(block_parts(k), node_a[:, n % 2, :], node_r[:, 0, :]).then_inc(s_nf, 1)

            def find_last(k):
                dve.wait_ge(s_rowg[k % 2], 16 * (k // 2 + 1))
                if k:
                    dve.wait_ge(s_rowd, k)
                link(dve.tensor_scalar(row_junk[:, :], row_dst[:, k % 2, :], node_id[:, k:k + 1], 0.0,
                                       ALU.is_le, ALU.add, accum_out=last_edge_f[:, k:k + 1]))
                dve.tensor_scalar(row_junk[:, :], row_dst[:, k % 2, :], node_id[:, k:k + 1], 0.0,
                                  ALU.is_equal, ALU.add, accum_out=in_row[:, k:k + 1]).then_inc(s_rowd, 1)

            for l in range(LAYERS):
                node_stage(l)
                onehots(l * N_TILES)
                for t in range(N_TILES):
                    T = l * N_TILES + t
                    if t + 1 < N_TILES:
                        onehots(T + 1)
                    C = l * N_CHUNKS + t // CHUNK
                    o = (t % CHUNK) * TILE
                    if t % CHUNK == 0:
                        dve.wait_ge(s_chunk[C % 2], chunk_count(C))
                    dve.wait_ge(s_h, T + 1)
                    if T >= 3:
                        dve.wait_ge(s_tr, T - 2)
                    if T:
                        dve.wait_ge(s_scan, T)
                    dve.tensor_tensor_scan(running[:, T % 3, :], cap_all[:, C % 2, o:o + TILE], ps_h[T % 2][:, :],
                                           running[:, (T - 1) % 3, TILE - 1:TILE] if t else 0.0,
                                           ALU.min, ALU.max).then_inc(s_scan, 1)
                    if l == 0 and t % SIDE == 6 and t // SIDE < N_BLOCKS:
                        find_last(t // SIDE)
                if l == 0:
                    dve.wait_ge(s_rowd, N_BLOCKS)
                    link(dve.tensor_scalar(row_count[:, :], row_count[:, :], float(TILE), -1.0, ALU.mult, ALU.add))
                    link(dve.tensor_tensor(last_edge_f[:, :], last_edge_f[:, :], row_count[:, :], ALU.add))
                    link(dve.tensor_scalar(last_edge_f[:, :], last_edge_f[:, :], 0.0, None, ALU.max))
                    link(dve.tensor_scalar(has_edge[:, :], in_row[:, :], 1.0, None, ALU.min))
                    dve.tensor_copy(last_edge[:, :], last_edge_f[:, :]).then_inc(s_ends, 1)

            for k in range(N_BLOCKS):
                aggregate(LAYERS, k)
                link(layernorm(h_nodes[:, k, :], node_a[:, 0, :]))
                dve.tensor_tensor_reduce(out=node_r[:, 1, :], in0=h_nodes[:, k, :], in1=att_all[:, 0, :], scale=1.0,
                                         scalar=0.0, op0=ALU.mult, op1=ALU.add, accum_out=s_node[:, k:k + 1])
                dve.tensor_tensor_reduce(out=node_v[:, 0, :], in0=h_nodes[:, k, :], in1=att_all[:, 1, :], scale=1.0,
                                         scalar=0.0, op0=ALU.mult, op1=ALU.add, accum_out=t_node[:, k:k + 1])
                link(split(block_parts(k), h_nodes[:, k, :], node_r[:, 0, :]))
                dve.tensor_copy(stats[:, 0:1], mv[:, 0:1]).then_inc(s_hn, 1)
                dve.tensor_copy(stats[:, 1:2], mv[:, 0:1]).then_inc(s_nv, 1)
            split([s_parts[:, j, :] for j in range(PARTS)], s_node[:, :], tmp_node[:, 0, :])
            tp = t_parts[:, 0:N_BLOCKS * PARTS].rearrange("p (b j) -> p b j", j=PARTS)
            split([tp[:, :, j] for j in range(PARTS)], t_node[:, :], tmp_node[:, 1, :]).then_inc(s_hn, 1)

            def flush(fb):
                t0, t1 = fb * FLUSH, min((fb + 1) * FLUSH, N_TILES)
                dve.wait_ge(s_sc, t1)
                n = (t1 - t0) * GPT
                dve.tensor_reduce(score[:, t0 * GPT:t1 * GPT], ps_t[fb % 2][:, 0:4 * n].rearrange("p (n j) -> p n j", j=4),
                                  AX.X, ALU.add).then_inc(s_fl, 1)

            T0 = LAYERS * N_TILES
            flushed = 0
            for t in range(N_TILES + 1):
                if t < N_TILES:
                    onehots(T0 + t)
                    dve.wait_ge(s_lo, t + 1)
                    if t >= 2:
                        dve.wait_ge(s_pick, t - 1)
                    dve.tensor_scalar(lo_onehot[:, t % 2, :], ps_z[0][:, :], part_id[:, 0:1], None,
                                      ALU.is_equal).then_inc(s_loh, 1)
                if t >= 1:
                    u = t - 1
                    dve.wait_ge(s_hi, u + 1)
                    dve.wait_ge(s_pickc, u + 1)
                    if u >= 2:
                        dve.wait_ge(s_sc, u - 1)
                    dve.scalar_tensor_tensor(out=s_masked[:, u % 2, :], in0=ps_z[1][0:N_BLOCKS, :],
                                             scalar=part_id[0:N_BLOCKS, 0:1], in1=s_picked[:, u % 2, :],
                                             op0=ALU.is_equal, op1=ALU.mult).then_inc(s_msk, 1)
                    if u % FLUSH == FLUSH // 2 and u > FLUSH:
                        flush(u // FLUSH - 1)
                        flushed = u // FLUSH
            for fb in range(flushed, -(-N_TILES // FLUSH)):
                flush(fb)
            dve.wait_ge(s_fl, -(-N_TILES // FLUSH))
            link(dve.scalar_tensor_tensor(out=score[:, :], in0=score[:, :], scalar=SLOPE, in1=score[:, :],
                                          op0=ALU.mult, op1=ALU.max))
            edges_last = N_EDGES - (N_GROUPS - 1) * GROUP
            link(dve.tensor_scalar(pad_cap[:, :], part_id[:, 0:1], float(edges_last), None, ALU.is_lt))
            link(dve.tensor_scalar(pad_cap[:, :], pad_cap[:, :], 2.0, -1.0, ALU.mult, ALU.add))
            link(dve.tensor_scalar(pad_cap[:, :], pad_cap[:, :], BIG, None, ALU.mult))
            link(dve.tensor_tensor(score[:, N_GROUPS - 1:], score[:, N_GROUPS - 1:], pad_cap[:, :], ALU.min))
            dve.tensor_reduce(soft[:, 0:1], score[:, :], AX.X, ALU.max).then_inc(s_red, 1)
            dve.wait_ge(s_all, 1)
            dve.tensor_scalar(soft[:, 2:3], soft[:, 1:2], -1.0, None, ALU.mult).then_inc(s_red, 1)
            dve.wait_ge(s_exp, 1)
            link(dve.tensor_tensor(coef[:, :], coef[:, :], score[:, :], ALU.mult))
            dve.wait_ge(s_all, 2)
            link(dve.reciprocal(soft[:, 5:6], soft[:, 4:5]))

            T1 = T0 + N_TILES
            spare = soft[:, 0:1]
            link(dve.tensor_scalar(spare, part_id[:, 0:1], float(N_PAD), None, ALU.add))
            link(dve.tensor_scalar(score[:, :], src_f[:, :], spare, None, ALU.subtract))
            for t in range(N_TILES):
                onehots(T1 + t)
                dve.wait_ge(s_hi, N_TILES + t + 1)
                if t >= 2:
                    dve.wait_ge(s_ms, t - 1)
                for g in range(GPT):
                    i = t * GPT + g
                    row = ps_t[t % 2][:, g * GROUP:(g + 1) * GROUP]
                    dve.scalar_tensor_tensor(out=dup_scratch[:, g, :], in0=row, scalar=src_f[:, i:i + 1],
                                             in1=strict_lower[:, :], op0=ALU.is_equal, op1=ALU.mult,
                                             accum_out=dup_count[:, t % 2, g:g + 1])
                    last = dve.tensor_scalar(same_src[:, t % 2, g, :], row, src_f[:, i:i + 1], coef[:, i:i + 1],
                                             ALU.is_equal, ALU.mult)
                last.then_inc(s_same, 1)
                dve.wait_ge(s_same, t + 1)
                link(dve.scalar_tensor_tensor(out=dup_pick[:, :], in0=dup_count[:, t % 2, :], scalar=0.0,
                                              in1=score[:, t * GPT:(t + 1) * GPT], op0=ALU.is_equal, op1=ALU.mult))
                if t >= 4:
                    for a in range(ACCS):
                        dve.wait_ge(s_acc[a], acc_count(a, (t - 3) * GPT))
                dve.tensor_scalar(scatter_row[:, t % 4, :], dup_pick[:, :], spare, None, ALU.add).then_inc(s_idx, 1)

            for k in range(N_BLOCKS // FIN):
                dve.wait_ge(s_fin[k % 2], 16 * ACCS * (k // 2 + 1))
                a = [acc_in(k % 2, i) for i in range(ACCS)]
                dve.tensor_tensor(a[0], a[0], a[1], ALU.add)
                link(dve.tensor_tensor(a[2], a[2], a[3], ALU.add))
                link(dve.tensor_tensor(a[0], a[0], a[2], ALU.add))
                hb = h_nodes[:, k * FIN:(k + 1) * FIN, :]
                link(dve.scalar_tensor_tensor(out=a[1], in0=a[0], scalar=soft[:, 5:6], in1=hb,
                                              op0=ALU.mult, op1=ALU.add))
                for b in range(FIN):
                    last = layernorm(h_nodes[:, k * FIN + b, :], a[1][:, b, :])
                    link(last)
                dve.tensor_copy(stats[:, 0:1], mv[:, 0:1]).then_inc(s_fd, 1)


_SUF = ("in", "hid", "out")


def kernel(x, src, dst, edge_weight, **w):
    import numpy as np
    import concourse.bacc as bacc
    from concourse.bass_utils import run_bass_kernel_spmd

    def cols(a):
        full = np.zeros((E_PAD,), a.dtype)
        full[:N_EDGES] = a
        return np.ascontiguousarray(full.reshape(N_GROUPS, GROUP).T)

    x, src, dst, edge_weight = (np.asarray(a) for a in (x, src, dst, edge_weight))
    dst_line = np.full((E_PAD,), N_NODES, dst.dtype)
    dst_line[:N_EDGES] = dst
    dst_before_line = np.concatenate([np.full((1,), -1, dst.dtype), dst_line[:-1]])
    src_line = np.zeros((E_PAD,), src.dtype)
    src_line[:N_EDGES] = src
    arrays = {"x": x, "src_cols": cols(src), "ew_cols": cols(edge_weight), "dst_line": dst_line, "dst_before_line": dst_before_line, "src_line": src_line,
              "group_heads": np.ascontiguousarray(dst_line[::GROUP]), "tile_heads": np.ascontiguousarray(dst_line[::TILE])}
    for s in _SUF:
        for k in ("W1", "b1", "W2", "b2"):
            arrays[f"{k}_{s}"] = np.asarray(w[f"L0_gnn_{k}_{s}"])
    arrays["att"] = np.asarray(w["L1_gnn_att"])

    nc = bacc.Bacc("TRN2", target_bir_lowering=False, num_devices=1)
    ap = {k: nc.dram_tensor(k, a.shape, mybir.dt.from_np(a.dtype), kind="ExternalInput").ap() for k, a in arrays.items()}
    out = nc.dram_tensor("result", (N_NODES, D), F32, kind="ExternalOutput").ap()
    build(nc, ap["x"], ap["src_cols"], ap["ew_cols"], ap["dst_line"], ap["dst_before_line"], ap["src_line"], ap["group_heads"], ap["tile_heads"],
          [ap[f"W1_{s}"] for s in _SUF], [ap[f"W2_{s}"] for s in _SUF], [ap[f"b1_{s}"] for s in _SUF],
          [ap[f"b2_{s}"] for s in _SUF], ap["att"], out)
    r = run_bass_kernel_spmd(nc, [arrays], core_ids=[0])
    return r.results[0]["result"]
```

```python
from contextlib import ExitStack

import concourse.bass as bass
from concourse import mybir

F32, BF16, I32 = mybir.dt.float32, mybir.dt.bfloat16, mybir.dt.int32
ALU = mybir.AluOpType
ACT = mybir.ActivationFunctionType
AX = mybir.AxisListType

P = 128
D = 128
N_NODES, N_EDGES = 6250, 206250
GROUP = P
TILE = 512
GPT = TILE // GROUP
N_TILES = -(-N_EDGES // TILE)
N_GROUPS = N_TILES * GPT
E_PAD = N_TILES * TILE
N_BLOCKS = -(-N_NODES // P)
N_PAD = N_BLOCKS * P
FULL_BLOCKS = N_NODES // P
TAIL_NODES = N_NODES - FULL_BLOCKS * P
PARTS = 3
BLOCK_COLS = PARTS * D
SPAN = (TILE - 1) // P + 2
ROW_GROUPS = 13
ROW_PARTS = N_GROUPS // ROW_GROUPS
CHUNK = 4
N_CHUNKS = -(-N_TILES // CHUNK)
LAYERS = 3
SIDE = 8
EPS = 1e-5
RING = 6
T_COLS = 96
SLOPE = 0.2
BIG = 3.2e38
ACCS = 4
ACC_ROWS = N_PAD + P
MAX_PE_GROUPS = 3
FIN = 7
assert ROW_PARTS * ROW_GROUPS == N_GROUPS and ROW_PARTS <= P and N_BLOCKS % FIN == 0


def build(nc, x, src_cols, ew_cols, dst_line, dst_before_line, src_line, tile_heads, tile_tails,
          w1, w2, b1, b2, att, out):
    ctx = ExitStack()
    with ctx:
        def sb(name, shape, dt=F32):
            return ctx.enter_context(nc.sbuf_tensor(name, shape, dt))

        def sem(name):
            return ctx.enter_context(nc.semaphore(name))

        def dram(name, shape, dt=F32):
            return nc.dram_tensor(name, shape, dt, kind="Internal").ap()

        b_table = dram("b_table", [N_PAD, D])
        prefix_max = dram("prefix_max", [E_PAD, D])
        dst_hi_line = dram("dst_hi_line", [ROW_PARTS, ROW_GROUPS * GROUP], BF16)
        dst_lo_line = dram("dst_lo_line", [ROW_PARTS, ROW_GROUPS * GROUP], BF16)
        cap_line = dram("cap_line", [ROW_PARTS, ROW_GROUPS * GROUP], BF16)
        lo_line = dram("lo_line", [ROW_PARTS, ROW_GROUPS * GROUP], BF16)
        hi_line = dram("hi_line", [ROW_PARTS, ROW_GROUPS * GROUP], BF16)
        s_table = dram("s_table", [N_PAD, 1])
        acc = [dram(f"acc{i}", [ACC_ROWS, D]) for i in range(ACCS)]

        def line(t):
            return t.rearrange("q n -> (q n)")

        src_i = sb("src_i", [P, N_GROUPS], I32)
        x_nodes = sb("x_nodes", [P, N_BLOCKS, D])
        h_nodes = sb("h_nodes", [P, N_BLOCKS, D])
        parts = sb("parts", [P, (N_BLOCKS + SPAN - 1) * BLOCK_COLS], BF16)
        tile_block = sb("tile_block", [1, 2, N_TILES], I32)
        ident = sb("ident", [P, P])
        lower = sb("lower", [P, P])
        part_id = sb("part_id", [P, 1])
        part_id_i = sb("part_id_i", [P, 1], I32)
        first_node = sb("first_node", [P, N_TILES])
        node_id = sb("node_id", [P, N_BLOCKS])
        node_id_i = sb("node_id_i", [P, N_BLOCKS], I32)
        last_edge = sb("last_edge", [P, N_BLOCKS], I32)
        last_edge_f = sb("last_edge_f", [P, N_BLOCKS])
        has_edge = sb("has_edge", [P, N_BLOCKS])
        row_of_node = sb("row_of_node", [P, N_BLOCKS], I32)
        row_count = sb("row_count", [P, N_BLOCKS])
        in_row = sb("in_row", [P, N_BLOCKS])
        w_in = sb("w_in", [P, LAYERS, 2, D])
        w_node = sb("w_node", [P, LAYERS, 2, D])
        w_out = sb("w_out", [P, LAYERS, D])
        b1_all = sb("b1_all", [P, LAYERS, D])
        b2_all = sb("b2_all", [P, LAYERS, D])
        att_all = sb("att_all", [P, 2, D])
        dst_row = sb("dst_row", [2, 2, CHUNK * TILE], BF16)
        cap_all = sb("cap_all", [P, 2, CHUNK * TILE], BF16)
        b_rows = sb("b_rows", [P, RING, GPT, D])
        onehot = sb("onehot", [P, 2 + SPAN - 1, TILE], BF16)
        z_relu = sb("z_relu", [P, 2, TILE])
        running = sb("running", [P, 3, TILE])
        run_rows = sb("run_rows", [P, 3, TILE])
        node_x = sb("node_x", [P, 4, D])
        node_v = sb("node_v", [P, 2, D])
        node_xT = sb("node_xT", [P, 2, P])
        node_a = sb("node_a", [P, 2, D])
        node_r = sb("node_r", [P, 2, D])
        node_b = sb("node_b", [P, 4, D])
        src_f = sb("src_f", [P, N_GROUPS])
        coef = sb("coef", [P, N_GROUPS])
        score = sb("score", [P, N_GROUPS])
        s_node = sb("s_node", [P, N_BLOCKS])
        t_node = sb("t_node", [P, N_BLOCKS])
        tmp_node = sb("tmp_node", [P, 2, N_BLOCKS])
        s_parts = sb("s_parts", [P, PARTS, N_BLOCKS], BF16)
        t_parts = sb("t_parts", [P, (N_BLOCKS + SPAN - 2) * PARTS + T_COLS], BF16)
        hilo_row = cap_all[0:2, :, :]
        sel_lo = sb("sel_lo", [2, P], BF16)
        sel_hi = sb("sel_hi", [2, P], BF16)
        sel_src = sb("sel_src", [2, P], BF16)
        sel_src_f = sb("sel_src_f", [2, 3, P])
        lo_onehot = sb("lo_onehot", [P, 2, TILE], BF16)
        src_hi = sb("src_hi", [P, N_GROUPS])
        hi_of_col = sb("hi_of_col", [P, PARTS * N_BLOCKS])
        hi_of_col_i = sb("hi_of_col_i", [P, PARTS * N_BLOCKS], I32)
        neg_part_id = sb("neg_part_id", [P, 1])
        s_src = b_rows[:, :, :, :].rearrange("p r g d -> p (r g d)")[:, 0:N_GROUPS]
        lo_distance = run_rows[:, 0:2, :]
        mask_scratch = running[:, 0:2, 0:MAX_PE_GROUPS * PARTS * N_BLOCKS]
        ones_col = sb("ones_col", [P, 1])
        stats = sb("stats", [P, FIN, 6])
        mean_var = sb("mean_var", [P, FIN, 2])
        rstd = sb("rstd", [P, 2, FIN])
        pad_cap = sb("pad_cap", [P, 1])
        soft = sb("soft", [P, 6])
        dup_count = sb("dup_count", [P, 2, GPT])
        dup_pick = sb("dup_pick", [P, GPT])
        scatter_row = sb("scatter_row", [P, RING, GPT], I32)

        ps_bc = [ctx.enter_context(nc.psum_tensor(f"ps_bc{i}", [P, TILE], F32)) for i in range(2)]
        ps_z = [ctx.enter_context(nc.psum_tensor(f"ps_z{i}", [P, TILE], F32)) for i in range(2)]
        ps_h = [ctx.enter_context(nc.psum_tensor(f"ps_h{i}", [P, TILE], F32)) for i in range(2)]
        ps_t = [ctx.enter_context(nc.psum_tensor(f"ps_t{i}", [P, TILE], F32)) for i in range(2)]

        last_rows = b_rows[:, :, :, :].rearrange("p r g d -> p (r g d)")[:, 0:3 * FIN * D].rearrange("p (r b d) -> p r b d", r=3, b=FIN)
        s_products = z_relu[:, :, :].rearrange("p r e -> p (r e)")[:, 0:FIN * D].rearrange("p (b d) -> p b d", d=D)
        split_rest = running[:, :, :].rearrange("p r e -> p (r e)")[:, 0:FIN * D].rearrange("p (b d) -> p b d", d=D)
        same_src = z_relu[:, :, :].rearrange("p r (g e) -> p r g e", g=GPT)

        s_in = sem("s_in")
        s_const = sem("s_const")
        s_prep = sem("s_prep")
        s_line = sem("s_line")
        s_x = sem("s_x")
        s_ready = sem("s_ready")
        s_chunk = [sem(f"s_chunk{i}") for i in range(2)]
        s_cap = [sem(f"s_cap{i}") for i in range(2)]
        s_bc = sem("s_bc")
        s_oh = sem("s_oh")
        s_g = [sem(f"s_g{i}") for i in range(RING)]
        s_z = sem("s_z")
        s_relu = sem("s_relu")
        s_h = sem("s_h")
        s_scan = sem("s_scan")
        s_tr = sem("s_tr")
        s_rr = sem("s_rr")
        s_st = [sem(f"s_st{i}") for i in range(3)]
        s_rowg = [sem(f"s_rowg{i}") for i in range(2)]
        s_rowd = sem("s_rowd")
        s_rowi = sem("s_rowi")
        s_ends = sem("s_ends")
        s_nx = [sem(f"s_nx{i}") for i in range(4)]
        s_nv = sem("s_nv")
        s_lr = [sem(f"s_lr{i}") for i in range(3)]
        s_nt = sem("s_nt")
        s_nc = sem("s_nc")
        s_nab = sem("s_nab")
        s_nf = sem("s_nf")
        s_nb = sem("s_nb")
        s_nst = [sem(f"s_nst{i}") for i in range(4)]
        s_dve = sem("s_dve")
        s_hn = sem("s_hn")
        s_sq = sem("s_sq")
        s_lo = sem("s_lo")
        s_loh = sem("s_loh")
        s_pick = sem("s_pick")
        s_loa = sem("s_loa")
        s_sd = sem("s_sd")
        s_trd = sem("s_trd")
        s_stt = sem("s_stt")
        s_stc = sem("s_stc")
        s_stab = sem("s_stab")
        s_sg = sem("s_sg")
        s_hi = sem("s_hi")
        s_tt = sem("s_tt")
        s_red = sem("s_red")
        s_all = sem("s_all")
        s_exp = sem("s_exp")
        s_coef = sem("s_coef")
        s_hl = [sem(f"s_hl{i}") for i in range(2)]
        s_zero = sem("s_zero")
        s_hx = sem("s_hx")
        s_hxc = sem("s_hxc")
        s_same = sem("s_same")
        s_idx = sem("s_idx")
        s_ms = sem("s_ms")
        s_msc = sem("s_msc")
        s_acc = [sem(f"s_acc{i}") for i in range(ACCS)]
        s_fin = [sem(f"s_fin{i}") for i in range(2)]
        s_fd = sem("s_fd")
        s_out = [sem(f"s_out{i}") for i in range(2)]

        N_IN = 16 * (8 + 5 * LAYERS)

        prep = h_nodes[:, :, :].rearrange("p b d -> p (b d)")
        L = ROW_GROUPS * GROUP
        prep_i = prep.bitcast(I32)
        dst_now = prep_i[0:ROW_PARTS, 0:L]
        dst_before = prep_i[0:ROW_PARTS, L:2 * L]
        src_now = prep_i[0:ROW_PARTS, 2 * L:3 * L]
        dst_hi_sb = parts[0:ROW_PARTS, 0:L]
        dst_lo_sb = parts[0:ROW_PARTS, L:2 * L]
        cap_sb = parts[0:ROW_PARTS, 2 * L:3 * L]
        hi_sb = parts[0:ROW_PARTS, 3 * L:4 * L]
        lo_sb = parts[0:ROW_PARTS, 4 * L:5 * L]
        digit_i = [parts[0:ROW_PARTS, (5 + 2 * j) * L:(7 + 2 * j) * L].bitcast(I32) for j in range(3)]
        same_f = parts[0:ROW_PARTS, 11 * L:12 * L]
        row_dst = prep_i[:, 3 * L:3 * L + 2 * TILE].rearrange("p (a e) -> p a e", a=2)
        row_junk = prep[:, 3 * L + 2 * TILE:].bitcast(BF16)[:, 0:TILE]
        dst_tiles = dst_line.rearrange("(t e) -> t e", e=TILE)
        src_hi_i = prep_i[:, 0:N_GROUPS]
        heads_i = score[:, 0:N_TILES].bitcast(I32)
        heads_f = score[:, N_TILES:2 * N_TILES]

        def gathered(l, i):
            return 16 * ((l * N_BLOCKS + 3 - i) // 4)

        def acc_count(a, n):
            return 16 * ((n + ACCS - 1 - a) // ACCS)

        def acc_in(slot, a):
            o = (slot * ACCS + a) * FIN * D
            return parts[:, :].bitcast(F32)[:, o:o + FIN * D].rearrange("p (b d) -> p b d", d=D)

        block = ctx.enter_context(nc.Block())

        def pe_groups(t):
            return MAX_PE_GROUPS if t % 4 == 3 else MAX_PE_GROUPS - 1

        def onehot_slot(T, q):
            return T % 2 if q == 0 else 1 + q

        def further_blocks(eng, more, work):
            with eng.If(more > 0):
                work(1)
                with eng.If(more > 1):
                    for q in range(2, SPAN):
                        work(q)

        def tiles_in(c):
            return min(CHUNK, N_TILES - c * CHUNK)

        def store_out(sp, k):
            sp.wait_ge(s_fd, k + 1)
            b0 = k * FIN
            full = min(FIN, FULL_BLOCKS - b0)
            sp.dma_start(out[b0 * P:(b0 + full) * P, :].rearrange("(b p) d -> p b d", p=P),
                         h_nodes[:, b0:b0 + full, :]).then_inc(s_out[k % 2], 16)
            if full < FIN:
                sp.dma_start(out[FULL_BLOCKS * P:N_NODES, :],
                             h_nodes[0:TAIL_NODES, FULL_BLOCKS, :]).then_inc(s_out[k % 2], 16)

        @block.sync
        def _(sp):
            def as_rows(t):
                return t.rearrange("(q n) -> q n", q=ROW_PARTS)

            sp.dma_start(dst_now, as_rows(dst_line)).then_inc(s_in, 16)
            sp.dma_start(dst_before, as_rows(dst_before_line)).then_inc(s_in, 16)
            sp.dma_start(src_now, as_rows(src_line)).then_inc(s_in, 16)
            sp.dma_start(heads_i[:, :], tile_heads.rearrange("(a n) -> a n", a=1).to_broadcast([P, N_TILES])).then_inc(s_in, 16)
            for j, t in enumerate((tile_heads, tile_tails)):
                sp.dma_start(tile_block[:, j, :], t.rearrange("(a n) -> a n", a=1)).then_inc(s_in, 16)
            sp.dma_start(src_i[:, :], src_cols).then_inc(s_in, 16)
            sp.dma_start(coef[:, :], ew_cols).then_inc(s_in, 16)
            for l in range(LAYERS):
                sp.dma_start(w_in[:, l, 0, :], w1[l][0:D, :]).then_inc(s_in, 16)
                sp.dma_start(w_in[:, l, 1, :], w1[l][D:2 * D, :]).then_inc(s_in, 16)
                sp.dma_start(w_out[:, l, :], w2[l]).then_inc(s_in, 16)
                sp.dma_start(b1_all[:, l, :], b1[l].rearrange("(a n) -> a n", a=1).to_broadcast([P, D])).then_inc(s_in, 16)
                sp.dma_start(b2_all[:, l, :], b2[l].rearrange("(a n) -> a n", a=1).to_broadcast([P, D])).then_inc(s_in, 16)
            for i in range(2):
                sp.dma_start(att_all[:, i, :], att[i * D:(i + 1) * D, :].rearrange("n a -> a n").to_broadcast([P, D])).then_inc(s_x, 16)
            sp.wait_ge(s_const, 1)
            sp.dma_start(x_nodes[:, 0:FULL_BLOCKS, :],
                         x[0:FULL_BLOCKS * P, :].rearrange("(b p) d -> p b d", p=P)).then_inc(s_x, 16)
            sp.dma_start(x_nodes[0:TAIL_NODES, FULL_BLOCKS, :], x[FULL_BLOCKS * P:N_NODES, :]).then_inc(s_x, 16)
            sp.wait_ge(s_prep, 1)
            for dst_t, s in ((dst_hi_line, dst_hi_sb), (dst_lo_line, dst_lo_sb),
                             (cap_line, cap_sb), (lo_line, lo_sb), (hi_line, hi_sb)):
                sp.dma_start(dst_t, s).then_inc(s_line, 16)
            sp.wait_ge(s_line, 80)
            for a in range(ACCS):
                for b0 in range(0, N_BLOCKS + 1, GPT):
                    nb = min(GPT, N_BLOCKS + 1 - b0)
                    sp.dma_start(acc[a][b0 * P:(b0 + nb) * P, :].rearrange("(b p) d -> p b d", p=P),
                                   run_rows[:, 0, 0:nb * D].rearrange("p (b d) -> p b d", d=D)).then_inc(s_zero, 16)

            def load_line(C, c, t, to, s):
                e0, n = c * CHUNK * TILE, tiles_in(c) * TILE
                sp.dma_start(to[:, C % 2, 0:n], line(t)[e0:e0 + n].rearrange("(a n) -> a n", a=1)
                             .to_broadcast([to.shape[0], n])).then_inc(s[C % 2], 16)

            def load_dst(C, c):
                load_line(C, c, dst_hi_line, dst_row[0:1, :, :], s_chunk)
                load_line(C, c, dst_lo_line, dst_row[1:2, :, :], s_chunk)

            def load_src(C, c):
                load_line(C, c, hi_line, hilo_row[0:1, :, :], s_hl)
                load_line(C, c, lo_line, hilo_row[1:2, :, :], s_hl)

            def store_b(l, k):
                n = l * N_BLOCKS + k
                sp.wait_ge(s_nb, n + 1)
                if l and not k:
                    sp.wait_ge(s_z, l * N_TILES)
                sp.dma_start(b_table[k * P:(k + 1) * P, :], node_b[:, n % 4, :]).then_inc(s_nst[n % 4], 16)

            for l in range(LAYERS):
                for k in range(N_BLOCKS):
                    store_b(l, k)
                for c in range(N_CHUNKS):
                    C = l * N_CHUNKS + c
                    if C >= 2:
                        before = (C - 1) // N_CHUNKS * N_TILES + (C - 1) % N_CHUNKS * CHUNK
                        sp.wait_ge(s_bc, before)
                    load_dst(C, c)
                    if C >= 2:
                        sp.wait_ge(s_scan, before)
                    load_line(C, c, cap_line, cap_all, s_cap)

            sp.wait_ge(s_stc, 1)
            sp.dma_start(s_table.rearrange("(b p) a -> b (p a)", p=P), node_b[0:N_BLOCKS, 0, :]).then_inc(s_stab, 16)
            for ph in range(2):
                for c in range(N_CHUNKS):
                    C = (LAYERS + ph) * N_CHUNKS + c
                    q = ph * N_CHUNKS + c
                    before = (C - 1) // N_CHUNKS * N_TILES + (C - 1) % N_CHUNKS * CHUNK
                    sp.wait_ge(s_bc, before)
                    load_dst(C, c)
                    if q >= 2:
                        done = before - LAYERS * N_TILES
                        sp.wait_ge(s_lo, min(done, N_TILES))
                        if done > N_TILES:
                            sp.wait_ge(s_hi, done - N_TILES)
                    elif q == 0:
                        sp.wait_ge(s_scan, LAYERS * N_TILES)
                    load_src(C, c)

            for i in range(ACCS):
                sp.wait_ge(s_acc[i], acc_count(i, N_GROUPS))
            for k in range(N_BLOCKS // FIN):
                if k >= 2:
                    sp.wait_ge(s_fd, k - 1)
                for i in range(ACCS):
                    sp.dma_start(acc_in(k % 2, i),
                                 acc[i][k * FIN * P:(k + 1) * FIN * P, :].rearrange("(b p) d -> p b d", p=P)).then_inc(s_fin[k % 2], 16)
                if k >= 1:
                    store_out(sp, k - 1)
            store_out(sp, N_BLOCKS // FIN - 1)
            for i in range(2):
                n_full = (N_BLOCKS // FIN + 1 - i) // 2
                extra = 1 if (N_BLOCKS // FIN - 1) % 2 == i else 0
                sp.wait_ge(s_out[i], 16 * (n_full + extra))

        @block.gpsimd
        def _(pool):
            pool.memset(x_nodes[:, FULL_BLOCKS, :], 0.0).then_inc(s_const, 1)
            pool.memset(ident[:, :], 0.0)
            pool.memset(lower[:, :], 1.0)
            pool.memset(ones_col[:, :], 1.0)
            pool.memset(run_rows[:, 0, :], 0.0)
            pool.memset(sel_src_f[:, :, :], 0.0).then_inc(s_const, 1)
            pool.wait_ge(s_const, 2)
            pool.affine_select(out=ident[:, :], in_=ident[:, :], compare_op=ALU.not_equal, fill=1.0,
                               base=0, pattern=[[-1, P]], channel_multiplier=1)
            pool.affine_select(out=lower[:, :], in_=lower[:, :], compare_op=ALU.is_ge, fill=0.0,
                               base=0, pattern=[[-1, P]], channel_multiplier=1)
            for j, (row, val) in enumerate(((1, 1.0), (0, 1.0), (1, 1.0))):
                pool.affine_select(out=sel_src_f[:, j, :], in_=sel_src_f[:, j, :], compare_op=ALU.not_equal, fill=val,
                                   base=-row, pattern=[[0, P]], channel_multiplier=1)
            pool.iota(part_id_i[:, :], pattern=[[P, 1]], base=0, channel_multiplier=1)
            pool.iota(hi_of_col_i[:, :], pattern=[[0, PARTS], [1, N_BLOCKS]], base=0, channel_multiplier=0)
            pool.iota(node_id_i[:, :], pattern=[[P, N_BLOCKS]], base=0, channel_multiplier=1).then_inc(s_const, 1)
            pool.wait_ge(s_const, 3)
            pool.affine_select(out=sel_src_f[:, 2, :], in_=sel_src_f[:, 2, :], compare_op=ALU.not_equal, fill=float(P),
                               base=0, pattern=[[0, P]], channel_multiplier=1).then_inc(s_const, 1)
            def row_gather(k):
                pool.wait_ge(s_rowi, 1)
                if k >= 2:
                    pool.wait_ge(s_rowd, k - 1)
                pool.indirect_dma_start(out=row_dst[:, k % 2, :], out_offset=None, in_=dst_tiles,
                                        in_offset=bass.IndirectOffsetOnAxis(ap=row_of_node[:, k:k + 1], axis=0)
                                        ).then_inc(s_rowg[k % 2], 16)

            def node_gather(l, k):
                n = (l - 1) * N_BLOCKS + k
                if n >= 4:
                    pool.wait_ge(s_nv, n - 3)
                pool.indirect_dma_start(out=node_x[:, n % 4, :], out_offset=None, in_=prefix_max,
                                        in_offset=bass.IndirectOffsetOnAxis(ap=last_edge[:, k:k + 1], axis=0)
                                        ).then_inc(s_nx[n % 4], 16)

            def last_gather(k):
                c, b = divmod(k, FIN)
                if c >= 3 and b == 0:
                    pool.wait_ge(s_hn, c - 2)
                pool.indirect_dma_start(out=last_rows[:, c % 3, b, :], out_offset=None, in_=prefix_max,
                                        in_offset=bass.IndirectOffsetOnAxis(ap=last_edge[:, k:k + 1], axis=0)
                                        ).then_inc(s_lr[c % 3], 16)

            pool.wait_ge(s_in, N_IN)
            for l in range(LAYERS):
                for i in range(4):
                    pool.wait_ge(s_nst[i], 16 * (((l + 1) * N_BLOCKS + 3 - i) // 4))
                for t in range(N_TILES):
                    T = l * N_TILES + t
                    if T >= RING:
                        pool.wait_ge(s_z, T - RING + 1)
                    for g in range(GPT):
                        i = t * GPT + g
                        pool.indirect_dma_start(out=b_rows[:, T % RING, g, :], out_offset=None, in_=b_table,
                                                in_offset=bass.IndirectOffsetOnAxis(ap=src_i[:, i:i + 1], axis=0)
                                                ).then_inc(s_g[T % RING], 16)
                    if l == 0 and t % SIDE == 3 and t // SIDE < N_BLOCKS:
                        row_gather(t // SIDE)
                for i in range(3):
                    pool.wait_ge(s_st[i], 16 * (((l + 1) * N_TILES + 2 - i) // 3))
                pool.wait_ge(s_ends, 1)
                for k in range(N_BLOCKS):
                    if l + 1 < LAYERS:
                        node_gather(l + 1, k)
                    else:
                        last_gather(k)

            pool.wait_ge(s_stab, 16)
            for t in range(N_TILES):
                for g in range(pe_groups(t), GPT):
                    i = t * GPT + g
                    pool.indirect_dma_start(out=s_src[:, i:i + 1], out_offset=None, in_=s_table,
                                            in_offset=bass.IndirectOffsetOnAxis(ap=src_i[:, i:i + 1], axis=0)
                                            ).then_inc(s_sg, 16)
            pool.wait_ge(s_red, 1)
            pool.partition_all_reduce(soft[:, 1:2], soft[:, 0:1], P, bass.bass_isa.ReduceOp.max).then_inc(s_all, 1)
            pool.wait_ge(s_exp, 1)
            pool.partition_all_reduce(soft[:, 4:5], soft[:, 3:4], P, bass.bass_isa.ReduceOp.add).then_inc(s_all, 1)
            pool.wait_ge(s_zero, 16 * ACCS * -(-(N_BLOCKS + 1) // GPT))
            for t in range(N_TILES):
                pool.wait_ge(s_idx, t + 1)
                pool.wait_ge(s_msc, t + 1)
                for g in range(GPT):
                    i = t * GPT + g
                    a = i % ACCS
                    if i >= ACCS:
                        pool.wait_ge(s_acc[a], acc_count(a, i))
                    pool.indirect_dma_start(out=acc[a],
                                            out_offset=bass.IndirectOffsetOnAxis(ap=scatter_row[:, t % RING, g:g + 1], axis=0),
                                            in_=b_rows[:, t % RING, g, :], in_offset=None,
                                            compute_op=ALU.add).then_inc(s_acc[a], 16)

        @block.tensor
        def _(pe):
            def broadcast_dst(T, t):
                C = T // N_TILES * N_CHUNKS + t // CHUNK
                if t % CHUNK == 0:
                    pe.wait_ge(s_chunk[C % 2], 32 * (C // 2 + 1))
                if T >= 2:
                    pe.wait_ge(s_oh, T - 1)
                o = (t % CHUNK) * TILE
                pe.matmul(ps_bc[T % 2][:, :], sel_src[:, :], dst_row[:, C % 2, o:o + TILE],
                          start=True, stop=True).then_inc(s_bc, 1)

            def window(t):
                return (pe.value_load(tile_block[0:1, 0, t:t + 1], min_val=0, max_val=N_BLOCKS - 1),
                        pe.value_load(tile_block[0:1, 1, t:t + 1], min_val=0, max_val=SPAN - 1))

            pe.wait_ge(s_const, 4)
            pe.wait_ge(s_ready, 1)
            pe.wait_ge(s_in, N_IN)
            for l in range(LAYERS):
                for k in range(N_BLOCKS + 1):
                    n = l * N_BLOCKS + k
                    if k < N_BLOCKS:
                        if l == 0:
                            pe.wait_ge(s_x, 64)
                            xin = x_nodes[:, k, :]
                        else:
                            m = n - N_BLOCKS
                            pe.wait_ge(s_nv, m + 1)
                            xin = node_v[:, m % 2, :]
                        if n >= 2:
                            pe.wait_ge(s_nc, n - 1)
                        pe.transpose(ps_z[n % 2][:, 0:P], xin, ident[:, :]).then_inc(s_nt, 1)
                    if k >= 1:
                        n -= 1
                        pe.wait_ge(s_nc, n + 1)
                        if n >= 2:
                            pe.wait_ge(s_nf, n - 1)
                            pe.wait_ge(s_nb, n - 1)
                        for bank, w in ((ps_h, 0), (ps_t, 1)):
                            last = pe.matmul(bank[n % 2][:, 0:D], node_xT[:, n % 2, :], w_node[:, l, w, :],
                                             start=True, stop=True)
                        last.then_inc(s_nab, 1)
                pe.wait_ge(s_nf, (l + 1) * N_BLOCKS)
                pe.wait_ge(s_nb, (l + 1) * N_BLOCKS)
                broadcast_dst(l * N_TILES, 0)
                for t in range(N_TILES + 2):
                    T = l * N_TILES + t
                    if t + 1 < N_TILES:
                        broadcast_dst(T + 1, t + 1)
                    if t < N_TILES:
                        first, more = window(t)
                        pe.wait_ge(s_oh, T + 1)
                        if T >= 2:
                            pe.wait_ge(s_relu, T - 1)
                        z = ps_z[T % 2]

                        def a_rows(q, part):
                            pe.matmul(z[:, :], parts[:, bass.ds(first * BLOCK_COLS + (q * PARTS + part) * D, D)],
                                      onehot[:, onehot_slot(T, q), :], start=(q == 0 and part == 0), stop=False)

                        for part in range(PARTS):
                            a_rows(0, part)
                        def a_block(q):
                            for part in range(PARTS):
                                a_rows(q, part)

                        further_blocks(pe, more, a_block)
                        pe.wait_ge(s_g[T % RING], 16 * GPT * (T // RING + 1))
                        for g in range(GPT):
                            last = pe.matmul(z[:, g * GROUP:(g + 1) * GROUP], b_rows[:, T % RING, g, :], ident[:, :],
                                             start=False, stop=(g == GPT - 1))
                        last.then_inc(s_z, 1)
                    if 1 <= t <= N_TILES:
                        u = T - 1
                        pe.wait_ge(s_relu, u + 1)
                        if u >= 2:
                            pe.wait_ge(s_scan, u - 1)
                        pe.matmul(ps_h[u % 2][:, :], w_out[:, l, :], z_relu[:, u % 2, :],
                                  start=True, stop=True).then_inc(s_h, 1)
                    if 2 <= t:
                        u = T - 2
                        pe.wait_ge(s_scan, u + 1)
                        if u >= 2:
                            pe.wait_ge(s_rr, u - 1)
                        for g in range(GPT):
                            last = pe.transpose(ps_t[u % 2][:, g * GROUP:(g + 1) * GROUP],
                                                running[:, u % 3, g * GROUP:(g + 1) * GROUP], ident[:, :])
                        last.then_inc(s_tr, 1)

            T0 = LAYERS * N_TILES
            pe.wait_ge(s_hn, N_BLOCKS // FIN + 1)

            def hl_wait(q, t):
                if t % CHUNK == 0:
                    pe.wait_ge(s_hl[(LAYERS * N_CHUNKS + q) % 2], 32 * (q // 2 + 1))

            pe.transpose(ps_z[0][0:N_BLOCKS, 0:P], s_node[:, :], ident[:, :]).then_inc(s_stt, 1)
            pe.wait_ge(s_stc, 1)

            def digits(t):
                c, o = t // CHUNK, (t % CHUNK) * TILE
                broadcast_dst(T0 + t, t)
                hl_wait(c, t)
                if t >= 2:
                    pe.wait_ge(s_loa, t - 1)
                pe.matmul(ps_z[t % 2][:, :], sel_lo[:, :], hilo_row[:, (LAYERS * N_CHUNKS + c) % 2, o:o + TILE],
                          start=True, stop=True).then_inc(s_lo, 1)

            digits(0)
            for t in range(N_TILES):
                if t + 1 < N_TILES:
                    digits(t + 1)
                first, more = window(t)
                at = pe.snap(first * PARTS)
                pe.wait_ge(s_oh, T0 + t + 1)
                if t >= 2:
                    pe.wait_ge(s_trd, t - 1)

                def t_rows(q, g):
                    return pe.matmul(ps_h[t % 2][:, g * T_COLS:(g + 1) * T_COLS],
                                     onehot[:, onehot_slot(T0 + t, q), g * GROUP:(g + 1) * GROUP],
                                     t_parts[:, bass.ds(at + q * PARTS, T_COLS)],
                                     start=(q == 0 and g == 0), stop=(q == 0 and g == GPT - 1))

                for g in range(GPT - 1):
                    t_rows(0, g)

                def t_block(q):
                    for g in range(GPT):
                        t_rows(q, g)

                further_blocks(pe, more, t_block)
                t_rows(0, GPT - 1).then_inc(s_tt, 1)
                pe.wait_ge(s_loh, t + 1)
                if t >= 2:
                    pe.wait_ge(s_sd, t - 1)
                for g in range(pe_groups(t)):
                    last = pe.matmul(ps_t[t % 2][:, g * PARTS * N_BLOCKS:(g + 1) * PARTS * N_BLOCKS],
                                     lo_onehot[:, t % 2, g * GROUP:(g + 1) * GROUP],
                                     s_parts[:, :, :].rearrange("p j b -> p (j b)"), start=True, stop=True)
                last.then_inc(s_pick, 1)

            T1 = T0 + N_TILES
            pe.wait_ge(s_sd, N_TILES)
            pe.wait_ge(s_trd, N_TILES)

            def edge_rows(t):
                c, o = t // CHUNK, (t % CHUNK) * TILE
                broadcast_dst(T1 + t, t)
                hl_wait(N_CHUNKS + c, t)
                if t >= 2:
                    pe.wait_ge(s_same, t - 1)
                pe.matmul(ps_t[t % 2][:, :], sel_src[:, :], hilo_row[:, ((LAYERS + 1) * N_CHUNKS + c) % 2, o:o + TILE],
                          start=True, stop=True).then_inc(s_hi, 1)

            edge_rows(0)
            for t in range(N_TILES + 1):
                if t + 1 < N_TILES:
                    edge_rows(t + 1)
                if t < N_TILES:
                    u = t
                    pe.wait_ge(s_oh, T1 + u + 1)
                    if u >= 2:
                        pe.wait_ge(s_hxc, u - 1)
                    first, more = window(u)
                    at = [pe.snap(first * BLOCK_COLS + part * D) for part in range(PARTS)]

                    def h_rows(q, g, part):
                        return pe.matmul(ps_z[u % 2][:, g * D:(g + 1) * D],
                                         onehot[:, onehot_slot(T1 + u, q), g * GROUP:(g + 1) * GROUP],
                                         parts[:, bass.ds(at[part] + q * BLOCK_COLS, D)],
                                         start=(q == 0 and g == 0 and part == 0),
                                         stop=(q == 0 and g == GPT - 1 and part == PARTS - 1))

                    order = [(g, part) for g in range(GPT) for part in range(PARTS)]
                    for g, part in order[:-PARTS]:
                        h_rows(0, g, part)

                    def h_block(q):
                        for g, part in order:
                            h_rows(q, g, part)

                    further_blocks(pe, more, h_block)
                    for g, part in order[-PARTS:]:
                        last = h_rows(0, g, part)
                    last.then_inc(s_hx, 1)
                if t >= 1:
                    u = t - 1
                    pe.wait_ge(s_hxc, u + 1)
                    pe.wait_ge(s_same, u + 1)
                    if u >= 2:
                        pe.wait_ge(s_msc, u - 1)
                    for g in range(GPT):
                        last = pe.matmul(ps_h[u % 2][:, g * D:(g + 1) * D], same_src[:, u % 2, g, :],
                                         running[:, u % 2, g * D:(g + 1) * D], start=True, stop=True)
                    last.then_inc(s_ms, 1)

        @block.scalar
        def _(act):
            for l in range(LAYERS):
                for k in range(N_BLOCKS + 1):
                    n = l * N_BLOCKS + k
                    if k < N_BLOCKS:
                        act.wait_ge(s_nt, n + 1)
                        if n >= 2:
                            act.wait_ge(s_nab, n - 1)
                        act.activation(node_xT[:, n % 2, :], ps_z[n % 2][:, 0:P], ACT.Copy).then_inc(s_nc, 1)
                    if k >= 1:
                        n -= 1
                        act.wait_ge(s_nab, n + 1)
                        if n >= 4:
                            act.wait_ge(s_nst[n % 4], 16 * (n // 4))
                        act.activation(node_b[:, n % 4, :], ps_t[n % 2][:, 0:D], ACT.Copy).then_inc(s_nb, 1)
                for t in range(N_TILES + 2):
                    T = l * N_TILES + t
                    if t < N_TILES:
                        act.wait_ge(s_z, T + 1)
                        if T >= 2:
                            act.wait_ge(s_h, T - 1)
                        act.activation(z_relu[:, T % 2, :], ps_z[T % 2][:, :], ACT.Relu).then_inc(s_relu, 1)
                    if t >= 2:
                        u = T - 2
                        act.wait_ge(s_tr, u + 1)
                        if u >= 3:
                            act.wait_ge(s_st[u % 3], 16 * (u // 3))
                        if u == 0:
                            act.wait_ge(s_zero, 16 * ACCS * -(-(N_BLOCKS + 1) // GPT))
                        act.activation(run_rows[:, u % 3, :], ps_t[u % 2][:, :], ACT.Copy).then_inc(s_rr, 1)
                        if l and t == 2:
                            for i in range(4):
                                act.wait_ge(s_nx[i], gathered(l, i))
                        act.wait_ge(s_rr, u + 1)
                        e0 = (t - 2) * TILE
                        act.dma_start(prefix_max[e0:e0 + TILE, :].rearrange("(g e) d -> e g d", g=GPT),
                                      run_rows[:, u % 3, :].rearrange("p (g d) -> p g d", g=GPT)).then_inc(s_st[u % 3], 16)
            for k in range(N_BLOCKS // FIN):
                act.wait_ge(s_sq, 2 * k + 1)
                act.activation(rstd[:, 0, :], mean_var[:, :, 1], ACT.Sqrt).then_inc(s_sq, 1)
            act.wait_ge(s_stt, 1)
            act.activation(node_b[0:N_BLOCKS, 0, :], ps_z[0][0:N_BLOCKS, 0:P], ACT.Copy).then_inc(s_stc, 1)
            for t in range(N_TILES):
                act.wait_ge(s_lo, t + 1)
                act.activation(lo_distance[:, t % 2, :], ps_z[t % 2][:, :], ACT.Abs, bias=neg_part_id[:, :], scale=1.0).then_inc(s_loa, 1)
                act.wait_ge(s_loa, t + 1)
                if t >= 2:
                    act.wait_ge(s_pick, t - 1)
                act.activation(lo_onehot[:, t % 2, :], lo_distance[:, t % 2, :], ACT.Relu, bias=ones_col[:, :],
                               scale=-1.0).then_inc(s_loh, 1)
            act.wait_ge(s_red, 2)
            act.activation(score[:, :], score[:, :], ACT.Exp, bias=soft[:, 2:3], scale=1.0,
                           accum_out=soft[:, 3:4]).then_inc(s_exp, 1)
            for t in range(N_TILES + 1):
                if t < N_TILES:
                    act.wait_ge(s_hx, t + 1)
                    if t >= 2:
                        act.wait_ge(s_ms, t - 1)
                    for g in range(GPT):
                        i = t * GPT + g
                        last = act.activation(running[:, t % 2, g * D:(g + 1) * D], ps_z[t % 2][:, g * D:(g + 1) * D],
                                              ACT.Copy, scale=coef[:, i:i + 1])
                    last.then_inc(s_hxc, 1)
                if t >= 1:
                    u = t - 1
                    act.wait_ge(s_ms, u + 1)
                    if u >= RING:
                        for a in range(ACCS):
                            act.wait_ge(s_acc[a], acc_count(a, (u - RING + 1) * GPT))
                    act.activation(b_rows[:, u % RING, :, :].rearrange("p g d -> p (g d)"), ps_h[u % 2][:, :],
                                   ACT.Copy).then_inc(s_msc, 1)
            for k in range(N_BLOCKS // FIN):
                act.wait_ge(s_sq, 2 * (N_BLOCKS // FIN + k) + 1)
                act.activation(rstd[:, 0, :], mean_var[:, :, 1], ACT.Sqrt).then_inc(s_sq, 1)

        @block.vector
        def _(dve):
            chained = [0]

            def link(ins):
                chained[0] += 1
                ins.then_inc(s_dve, 1)
                dve.wait_ge(s_dve, chained[0])

            dve.wait_ge(s_in, N_IN)
            dve.wait_ge(s_const, 4)
            g3 = lambda t: t.rearrange("q (g e) -> q g e", e=GROUP)
            dve.tensor_scalar(digit_i[0], dst_now, 7, None, ALU.logical_shift_right)
            dve.tensor_scalar(digit_i[1], dst_now, P - 1, None, ALU.bitwise_and)
            dve.tensor_scalar(digit_i[2], src_now, P - 1, None, ALU.bitwise_and)
            dve.tensor_scalar(tile_block[:, :, :], tile_block[:, :, :], 7, None, ALU.logical_shift_right)
            link(dve.tensor_tensor(same_f, dst_now, dst_before, ALU.is_equal))
            link(dve.tensor_scalar(same_f, same_f, 2.0, -1.0, ALU.mult, ALU.add))
            dve.tensor_scalar(cap_sb, same_f, BIG, None, ALU.mult)
            dve.tensor_copy(dst_hi_sb, digit_i[0])
            dve.tensor_copy(dst_lo_sb, digit_i[1])
            link(dve.tensor_copy(lo_sb, digit_i[2]))
            link(dve.tensor_scalar(digit_i[2], src_now, 7, None, ALU.logical_shift_right))
            dve.tensor_copy(hi_sb, digit_i[2]).then_inc(s_prep, 1)
            dve.tensor_copy(part_id[:, :], part_id_i[:, :])
            dve.tensor_scalar(neg_part_id[:, :], part_id_i[:, :], -1.0, None, ALU.mult)
            dve.tensor_copy(hi_of_col[:, :], hi_of_col_i[:, :])
            dve.tensor_copy(node_id[:, :], node_id_i[:, :])
            link(dve.tensor_scalar(src_hi_i, src_i[:, :], 7, None, ALU.logical_shift_right))
            link(dve.tensor_copy(src_hi[:, :], src_hi_i))
            dve.tensor_copy(src_f[:, :], src_i[:, :])
            dve.tensor_copy(sel_lo[:, :], sel_src_f[:, 0, :])
            dve.tensor_copy(sel_hi[:, :], sel_src_f[:, 1, :])
            dve.tensor_copy(sel_src[:, :], sel_src_f[:, 2, :])
            dve.tensor_tensor(tile_block[:, 1, :], tile_block[:, 1, :], tile_block[:, 0, :], ALU.subtract)
            for l in range(LAYERS):
                dve.tensor_tensor(w_node[:, l, 0, :], w_in[:, l, 0, :], w_in[:, l, 1, :], ALU.subtract)
                dve.tensor_copy(w_node[:, l, 1, :], w_in[:, l, 1, :])
            dve.wait_ge(s_line, 80)
            dve.memset(t_parts[:, N_BLOCKS * PARTS:], 0.0)
            link(dve.memset(parts[:, N_BLOCKS * BLOCK_COLS:], 0.0))
            link(dve.tensor_copy(heads_f[:, :], heads_i[:, :]))
            link(dve.tensor_scalar(heads_i[:, :], heads_i[:, :], 7, 7, ALU.logical_shift_right, ALU.logical_shift_left))
            dve.tensor_scalar(first_node[:, :], heads_i[:, :], part_id[:, 0:1], None, ALU.add)
            for k in range(N_BLOCKS):
                link(dve.tensor_scalar(row_junk[:, 0:N_TILES], heads_f[:, :], node_id[:, k:k + 1], 0.0,
                                       ALU.is_le, ALU.add, accum_out=row_count[:, k:k + 1]))
            link(dve.tensor_scalar(row_count[:, :], row_count[:, :], -1.0, 0.0, ALU.add, ALU.max))
            dve.tensor_copy(row_of_node[:, :], row_count[:, :]).then_inc(s_rowi, 1)
            dve.tensor_copy(soft[:, 0:1], part_id[:, 0:1]).then_inc(s_ready, 1)

            def onehots(T):
                dve.wait_ge(s_bc, T + 1)
                if T >= 2:
                    onehot_used(T - 2)
                t = T % N_TILES

                def compare(q):
                    return dve.tensor_scalar(onehot[:, onehot_slot(T, q), :], ps_bc[T % 2][:, :], -float(q * P),
                                             first_node[:, t:t + 1], ALU.add, ALU.is_equal)

                more = dve.value_load(tile_block[0:1, 1, t:t + 1], min_val=0, max_val=SPAN - 1)

                def compare_block(q):
                    if T and q == 1:
                        onehot_used(T - 1)
                    compare(q)

                further_blocks(dve, more, compare_block)
                compare(0).then_inc(s_oh, 1)

            def onehot_used(u):
                ph, _ = divmod(u, N_TILES)
                if ph < LAYERS:
                    dve.wait_ge(s_z, u + 1)
                elif ph == LAYERS:
                    dve.wait_ge(s_tt, u + 1 - LAYERS * N_TILES)
                else:
                    dve.wait_ge(s_hx, u + 1 - (LAYERS + 1) * N_TILES)

            def split(dst3, val, rest, link_first=True):
                link(dve.tensor_copy(dst3[0], val))
                link(dve.tensor_tensor(rest, val, dst3[0], ALU.subtract))
                link(dve.tensor_copy(dst3[1], rest))
                return dve.tensor_tensor(dst3[2], rest, dst3[1], ALU.subtract)

            def block_parts(k):
                return [parts[:, k * BLOCK_COLS + j * D:k * BLOCK_COLS + (j + 1) * D] for j in range(PARTS)]

            def aggregate(l, k):
                m = (l - 1) * N_BLOCKS + k
                dve.wait_ge(s_nx[m % 4], 16 * (m // 4 + 1))
                link(dve.tensor_tensor(node_x[:, m % 4, :], node_x[:, m % 4, :], b2_all[:, l - 1, :], ALU.add))
                if m >= 2:
                    dve.wait_ge(s_nt, N_BLOCKS + m - 1)
                dve.tensor_scalar(node_v[:, m % 2, :], node_x[:, m % 4, :], has_edge[:, k:k + 1], 0.0,
                                  ALU.mult, ALU.max).then_inc(s_nv, 1)

            sq = [0]

            def layernorm(dst, val):
                for b in range(FIN):
                    last = dve.bn_stats(stats[:, b, :], val[:, b, :])
                link(last)
                for b in range(FIN):
                    last = dve.bn_aggr(mean_var[:, b, :], stats[:, b, :])
                link(last)
                dve.tensor_scalar(mean_var[:, :, 1], mean_var[:, :, 1], EPS, None, ALU.add).then_inc(s_sq, 1)
                sq[0] += 2
                dve.wait_ge(s_sq, sq[0])
                link(dve.reciprocal(rstd[:, 1, :], rstd[:, 0, :]))
                for b in range(FIN):
                    last = dve.tensor_scalar(dst[:, b, :], val[:, b, :], mean_var[:, b, 0:1], rstd[:, 1, b:b + 1],
                                             ALU.subtract, ALU.mult)
                return last

            def node_stage(l):
                for k in range(N_BLOCKS):
                    n = l * N_BLOCKS + k
                    if l:
                        aggregate(l, k)
                    if k >= 1:
                        finish_a(l, k - 1)
                finish_a(l, N_BLOCKS - 1)

            def finish_a(l, k):
                n = l * N_BLOCKS + k
                dve.wait_ge(s_nab, n + 1)
                link(dve.tensor_tensor(node_a[:, n % 2, :], ps_h[n % 2][:, 0:D], b1_all[:, l, :], ALU.add))
                if l and k == 0:
                    dve.wait_ge(s_z, l * N_TILES)
                split(block_parts(k), node_a[:, n % 2, :], node_r[:, 0, :]).then_inc(s_nf, 1)

            def find_last(k):
                dve.wait_ge(s_rowg[k % 2], 16 * (k // 2 + 1))
                if k:
                    dve.wait_ge(s_rowd, k)
                link(dve.tensor_scalar(row_junk[:, :], row_dst[:, k % 2, :], node_id[:, k:k + 1], 0.0,
                                       ALU.is_le, ALU.add, accum_out=last_edge_f[:, k:k + 1]))
                dve.tensor_scalar(row_junk[:, :], row_dst[:, k % 2, :], node_id[:, k:k + 1], 0.0,
                                  ALU.is_equal, ALU.add, accum_out=in_row[:, k:k + 1]).then_inc(s_rowd, 1)

            for l in range(LAYERS):
                node_stage(l)
                onehots(l * N_TILES)
                for step in range(N_TILES + 1):
                    if step + 1 < N_TILES:
                        onehots(l * N_TILES + step + 1)
                    if step == 0:
                        continue
                    t = step - 1
                    T = l * N_TILES + t
                    C = l * N_CHUNKS + t // CHUNK
                    o = (t % CHUNK) * TILE
                    if t % CHUNK == 0:
                        dve.wait_ge(s_cap[C % 2], 16 * (C // 2 + 1))
                    dve.wait_ge(s_h, T + 1)
                    if T >= 3:
                        dve.wait_ge(s_tr, T - 2)
                    if T:
                        dve.wait_ge(s_scan, T)
                    dve.tensor_tensor_scan(running[:, T % 3, :], cap_all[:, C % 2, o:o + TILE], ps_h[T % 2][:, :],
                                           running[:, (T - 1) % 3, TILE - 1:TILE] if t else 0.0,
                                           ALU.min, ALU.max).then_inc(s_scan, 1)
                    if l == 0 and t % SIDE == 6 and t // SIDE < N_BLOCKS:
                        find_last(t // SIDE)
                if l == 0:
                    dve.wait_ge(s_rowd, N_BLOCKS)
                    link(dve.tensor_scalar(row_count[:, :], row_count[:, :], float(TILE), -1.0, ALU.mult, ALU.add))
                    link(dve.tensor_tensor(last_edge_f[:, :], last_edge_f[:, :], row_count[:, :], ALU.add))
                    link(dve.tensor_scalar(last_edge_f[:, :], last_edge_f[:, :], 0.0, None, ALU.max))
                    link(dve.tensor_scalar(has_edge[:, :], in_row[:, :], 1.0, None, ALU.min))
                    dve.tensor_copy(last_edge[:, :], last_edge_f[:, :]).then_inc(s_ends, 1)

            def over_blocks(t):
                return t.rearrange("p (b d) -> p b d", b=1).to_broadcast([P, FIN, D])

            for c in range(N_BLOCKS // FIN):
                bs = slice(c * FIN, (c + 1) * FIN)
                rows = last_rows[:, c % 3, :, :]
                dve.wait_ge(s_lr[c % 3], 16 * FIN * (c // 3 + 1))
                link(dve.tensor_tensor(rows, rows, over_blocks(b2_all[:, LAYERS - 1, :]), ALU.add))
                link(dve.tensor_tensor(rows, rows, has_edge[:, bs].rearrange("p (b a) -> p b a", a=1)
                                       .to_broadcast([P, FIN, D]), ALU.mult))
                link(dve.tensor_tensor(rows, rows, x_nodes[:, bs, :], ALU.add))
                link(layernorm(h_nodes[:, bs, :], rows))
                for b in range(FIN):
                    k = c * FIN + b
                    dve.tensor_tensor_reduce(out=s_products[:, b, :], in0=h_nodes[:, k, :], in1=att_all[:, 0, :], scale=1.0,
                                             scalar=0.0, op0=ALU.mult, op1=ALU.add, accum_out=s_node[:, k:k + 1])
                    last = dve.tensor_tensor_reduce(out=rows[:, b, :], in0=h_nodes[:, k, :], in1=att_all[:, 1, :], scale=1.0,
                                                    scalar=0.0, op0=ALU.mult, op1=ALU.add, accum_out=t_node[:, k:k + 1])
                link(last)
                blocks = parts[:, c * FIN * BLOCK_COLS:(c + 1) * FIN * BLOCK_COLS].rearrange("p (b j d) -> p b j d", b=FIN, j=PARTS)
                split([blocks[:, :, j, :] for j in range(PARTS)], h_nodes[:, bs, :], split_rest).then_inc(s_hn, 1)
                dve.wait_ge(s_hn, c + 1)
            split([s_parts[:, j, :] for j in range(PARTS)], s_node[:, :], tmp_node[:, 0, :])
            tp = t_parts[:, 0:N_BLOCKS * PARTS].rearrange("p (b j) -> p b j", j=PARTS)
            split([tp[:, :, j] for j in range(PARTS)], t_node[:, :], tmp_node[:, 1, :]).then_inc(s_hn, 1)

            T0 = LAYERS * N_TILES
            onehots(T0)
            for t in range(N_TILES):
                if t + 1 < N_TILES:
                    onehots(T0 + t + 1)
                dve.wait_ge(s_tt, t + 1)
                dve.tensor_reduce(score[:, t * GPT:(t + 1) * GPT],
                                  ps_h[t % 2][:, 0:GPT * T_COLS].rearrange("p (g j) -> p g j", g=GPT)[:, :, 0:PARTS],
                                  AX.X, ALU.add).then_inc(s_trd, 1)
                dve.wait_ge(s_pick, t + 1)
                if t >= 2:
                    dve.wait_ge(s_sd, t - 1)
                for g in range(pe_groups(t)):
                    i = t * GPT + g
                    cols = slice(g * PARTS * N_BLOCKS, (g + 1) * PARTS * N_BLOCKS)
                    last = dve.scalar_tensor_tensor(out=mask_scratch[:, t % 2, cols], in0=hi_of_col[:, :],
                                                    scalar=src_hi[:, i:i + 1], in1=ps_t[t % 2][:, cols],
                                                    op0=ALU.is_equal, op1=ALU.mult, accum_out=s_src[:, i:i + 1])
                last.then_inc(s_sd, 1)
            dve.wait_ge(s_sd, N_TILES)
            dve.wait_ge(s_sg, 16 * sum(GPT - pe_groups(t) for t in range(N_TILES)))
            link(dve.tensor_tensor(score[:, :], score[:, :], s_src, ALU.add))
            link(dve.scalar_tensor_tensor(out=score[:, :], in0=score[:, :], scalar=SLOPE, in1=score[:, :],
                                          op0=ALU.mult, op1=ALU.max))
            edges_last = N_EDGES - (N_GROUPS - 1) * GROUP
            link(dve.tensor_scalar(pad_cap[:, :], part_id[:, 0:1], float(edges_last), None, ALU.is_lt))
            link(dve.tensor_scalar(pad_cap[:, :], pad_cap[:, :], 2.0, -1.0, ALU.mult, ALU.add))
            link(dve.tensor_scalar(pad_cap[:, :], pad_cap[:, :], BIG, None, ALU.mult))
            link(dve.tensor_tensor(score[:, N_GROUPS - 1:], score[:, N_GROUPS - 1:], pad_cap[:, :], ALU.min))
            dve.tensor_reduce(soft[:, 0:1], score[:, :], AX.X, ALU.max).then_inc(s_red, 1)
            dve.wait_ge(s_all, 1)
            dve.tensor_scalar(soft[:, 2:3], soft[:, 1:2], -1.0, None, ALU.mult).then_inc(s_red, 1)
            dve.wait_ge(s_exp, 1)
            link(dve.tensor_tensor(coef[:, :], coef[:, :], score[:, :], ALU.mult))
            dve.wait_ge(s_all, 2)
            link(dve.reciprocal(soft[:, 5:6], soft[:, 4:5]))

            T1 = T0 + N_TILES
            spare = soft[:, 0:1]
            link(dve.tensor_scalar(spare, part_id[:, 0:1], float(N_PAD), None, ALU.add))
            link(dve.tensor_scalar(score[:, :], src_f[:, :], spare, None, ALU.subtract))
            onehots(T1)
            for t in range(N_TILES):
                if t + 1 < N_TILES:
                    onehots(T1 + t + 1)
                dve.wait_ge(s_hi, t + 1)
                if t >= 2:
                    dve.wait_ge(s_ms, t - 1)
                for g in range(GPT):
                    i = t * GPT + g
                    last = dve.scalar_tensor_tensor(out=same_src[:, t % 2, g, :], in0=ps_t[t % 2][:, g * GROUP:(g + 1) * GROUP],
                                                    scalar=src_f[:, i:i + 1], in1=lower[:, :],
                                                    op0=ALU.is_equal, op1=ALU.mult, accum_out=dup_count[:, t % 2, g:g + 1])
                last.then_inc(s_same, 1)
                dve.wait_ge(s_same, t + 1)
                link(dve.scalar_tensor_tensor(out=dup_pick[:, :], in0=dup_count[:, t % 2, :], scalar=1.0,
                                              in1=score[:, t * GPT:(t + 1) * GPT], op0=ALU.is_equal, op1=ALU.mult))
                if t >= RING:
                    for a in range(ACCS):
                        dve.wait_ge(s_acc[a], acc_count(a, (t - RING + 1) * GPT))
                dve.tensor_scalar(scatter_row[:, t % RING, :], dup_pick[:, :], spare, None, ALU.add).then_inc(s_idx, 1)

            for k in range(N_BLOCKS // FIN):
                dve.wait_ge(s_fin[k % 2], 16 * ACCS * (k // 2 + 1))
                a = [acc_in(k % 2, i) for i in range(ACCS)]
                dve.tensor_tensor(a[0], a[0], a[1], ALU.add)
                link(dve.tensor_tensor(a[2], a[2], a[3], ALU.add))
                link(dve.tensor_tensor(a[0], a[0], a[2], ALU.add))
                hb = h_nodes[:, k * FIN:(k + 1) * FIN, :]
                link(dve.scalar_tensor_tensor(out=a[1], in0=a[0], scalar=soft[:, 5:6], in1=hb,
                                              op0=ALU.mult, op1=ALU.add))
                layernorm(hb, a[1]).then_inc(s_fd, 1)
                dve.wait_ge(s_fd, k + 1)


_SUF = ("in", "hid", "out")


def kernel(x, src, dst, edge_weight, **w):
    import numpy as np
    import concourse.bacc as bacc
    from concourse.bass_utils import run_bass_kernel_spmd

    def cols(a):
        full = np.zeros((E_PAD,), a.dtype)
        full[:N_EDGES] = a
        return np.ascontiguousarray(full.reshape(N_GROUPS, GROUP).T)

    x, src, dst, edge_weight = (np.asarray(a) for a in (x, src, dst, edge_weight))
    dst_line = np.full((E_PAD,), N_NODES, dst.dtype)
    dst_line[:N_EDGES] = dst
    dst_before_line = np.concatenate([np.full((1,), -1, dst.dtype), dst_line[:-1]])
    src_line = np.zeros((E_PAD,), src.dtype)
    src_line[:N_EDGES] = src
    arrays = {"x": x, "src_cols": cols(src), "ew_cols": cols(edge_weight), "dst_line": dst_line, "dst_before_line": dst_before_line, "src_line": src_line,
              "tile_heads": np.ascontiguousarray(dst_line[::TILE]), "tile_tails": np.ascontiguousarray(dst_line[TILE - 1::TILE])}
    for s in _SUF:
        for k in ("W1", "b1", "W2", "b2"):
            arrays[f"{k}_{s}"] = np.asarray(w[f"L0_gnn_{k}_{s}"])
    arrays["att"] = np.asarray(w["L1_gnn_att"])

    nc = bacc.Bacc("TRN2", target_bir_lowering=False, num_devices=1)
    ap = {k: nc.dram_tensor(k, a.shape, mybir.dt.from_np(a.dtype), kind="ExternalInput").ap() for k, a in arrays.items()}
    out = nc.dram_tensor("result", (N_NODES, D), F32, kind="ExternalOutput").ap()
    build(nc, ap["x"], ap["src_cols"], ap["ew_cols"], ap["dst_line"], ap["dst_before_line"], ap["src_line"], ap["tile_heads"], ap["tile_tails"],
          [ap[f"W1_{s}"] for s in _SUF], [ap[f"W2_{s}"] for s in _SUF], [ap[f"b1_{s}"] for s in _SUF],
          [ap[f"b2_{s}"] for s in _SUF], ap["att"], out)
    r = run_bass_kernel_spmd(nc, [arrays], core_ids=[0])
    return r.results[0]["result"]
```
